# Optimizing a Trainium2 kernel written in Bass

```python
import numpy as np
import jax
import jax.numpy as jnp

def _softmax(x, axis=-1):
    return jax.nn.softmax(x, axis=axis)

def _gelu(x):
    return jax.nn.gelu(x, approximate=True)

def _silu(x):
    return jax.nn.silu(x)

def _sigmoid(x):
    return jax.nn.sigmoid(x)

def _layernorm(x, axis=-1, eps=1e-05):
    m = jnp.mean(x, axis=axis, keepdims=True)
    v = jnp.var(x, axis=axis, keepdims=True)
    return (x - m) / jnp.sqrt(v + eps)

def _scatter_add(tgt, idx, src, axis=0):
    return tgt.at[idx].add(src)

def _segment_sum(src, seg, n):
    return jax.ops.segment_sum(src, seg, n)
kernel_name = 'mk_recurrent_d1_jaxref_r8_f99f9f'

def setup_inputs(seed: int=0):
    np.random.seed(seed)
    _w = jnp.asarray

    def _L0_attn_setup():
        import jax, jax.numpy as jnp
        import numpy as np
        B, S, E, H = (2, 256, 256, 16)
        D = E // H
        ROPE_BASE = 10000.0

        def rotate_half(x):
            x1 = x[..., ::2]
            x2 = x[..., 1::2]
            return jnp.stack((-x2, x1), axis=-1).reshape(x.shape[:-1] + (x.shape[-1],))

        def rope_cos_sin(seq_len, head_dim, start_pos=0):
            inv_freq = 1.0 / ROPE_BASE ** (jnp.arange(0, head_dim, 2, dtype=jnp.float32) / head_dim)
            positions = jnp.arange(start_pos, start_pos + seq_len, dtype=jnp.float32)
            freqs = jnp.outer(positions, inv_freq)
            emb = jnp.concatenate([freqs, freqs], axis=-1)
            return (emb[None, None].astype(jnp.float32), emb)
        key = jax.random.key(seed)
        k1, k2, k3 = jax.random.split(key, 3)
        x = jax.random.normal(k1, (B, S, E), dtype=jnp.float32)
        Wqkv = jax.random.normal(k2, (3 * E, E), dtype=jnp.float32) * E ** (-0.5)
        Wout = jax.random.normal(k3, (E, E), dtype=jnp.float32) * E ** (-0.5)
        return {'x': x, 'Wqkv': Wqkv, 'Wout': Wout}
    _L0_attn_in = _L0_attn_setup()

    def _L0_ffn_setup():
        import jax, jax.numpy as jnp
        import numpy as np
        NUM_ACT = 2
        key = jax.random.key(seed)
        k1, k2, k3, k4, k5 = jax.random.split(key, 5)
        B, S, D, I, E = (4, 64, 256, 512, 8)
        x = jax.random.normal(k1, (B, S, D), dtype=jnp.float32)
        gate_w = jax.random.normal(k2, (E, D), dtype=jnp.float32) * 0.02
        w1 = jax.random.normal(k3, (E, I, D), dtype=jnp.float32) * 0.02
        w2 = jax.random.normal(k4, (E, D, I), dtype=jnp.float32) * 0.02
        w3 = jax.random.normal(k5, (E, I, D), dtype=jnp.float32) * 0.02
        return {'x': x, 'gate_w': gate_w, 'w1': w1, 'w2': w2, 'w3': w3}
    _L0_ffn_in = _L0_ffn_setup()
    _d = {'L0_attn_x': _L0_attn_in['x'], 'L0_attn_Wqkv': _L0_attn_in['Wqkv'], 'L0_attn_Wout': _L0_attn_in['Wout'], 'L0_ffn_gate_w': _L0_ffn_in['gate_w'], 'L0_ffn_w1': _L0_ffn_in['w1'], 'L0_ffn_w2': _L0_ffn_in['w2'], 'L0_ffn_w3': _L0_ffn_in['w3']}
    _x0 = _d['L0_attn_x']
    _d['L0_attn_x'] = jax.random.normal(jax.random.fold_in(jax.random.key(seed), 1), (4, 1024, 256), dtype=_x0.dtype)
    del _x0
    return _d

def reference(L0_attn_x, L0_attn_Wqkv, L0_attn_Wout, L0_ffn_gate_w, L0_ffn_w1, L0_ffn_w2, L0_ffn_w3):

    def _L0_attn_ref(x, Wqkv, Wout):
        import jax, jax.numpy as jnp
        import numpy as np
        B, S, E, H = (2, 256, 256, 16)
        D = E // H
        ROPE_BASE = 10000.0

        def rotate_half(x):
            x1 = x[..., ::2]
            x2 = x[..., 1::2]
            return jnp.stack((-x2, x1), axis=-1).reshape(x.shape[:-1] + (x.shape[-1],))

        def rope_cos_sin(seq_len, head_dim, start_pos=0):
            inv_freq = 1.0 / ROPE_BASE ** (jnp.arange(0, head_dim, 2, dtype=jnp.float32) / head_dim)
            positions = jnp.arange(start_pos, start_pos + seq_len, dtype=jnp.float32)
            freqs = jnp.outer(positions, inv_freq)
            emb = jnp.concatenate([freqs, freqs], axis=-1)
            return (emb[None, None].astype(jnp.float32), emb)
        batch, seq_len, emb = x.shape
        scale = D ** (-0.5)
        qkv = x @ Wqkv.T
        qkv = qkv.reshape(batch, seq_len, 3, H, D)
        qkv = jnp.transpose(qkv, (2, 0, 3, 1, 4))
        q, k, v = (qkv[0], qkv[1], qkv[2])
        inv_freq = 1.0 / ROPE_BASE ** (jnp.arange(0, D, 2, dtype=jnp.float32) / D)
        positions = jnp.arange(seq_len, dtype=jnp.float32)
        freqs = jnp.outer(positions, inv_freq)
        emb_ang = jnp.concatenate([freqs, freqs], axis=-1)
        cos = jnp.cos(emb_ang)[None, None]
        sin = jnp.sin(emb_ang)[None, None]
        q = q * cos + rotate_half(q) * sin
        k = k * cos + rotate_half(k) * sin
        scores = jnp.einsum('bhqd,bhkd->bhqk', q, k) * scale
        causal = jnp.arange(seq_len)[None, :] > jnp.arange(seq_len)[:, None]
        scores = jnp.where(causal[None, None], -jnp.inf, scores)
        attn = jax.nn.softmax(scores, axis=-1)
        out = jnp.einsum('bhqk,bhkd->bhqd', attn, v)
        out = jnp.transpose(out, (0, 2, 1, 3)).reshape(batch, seq_len, emb)
        return out @ Wout.T

    def _L0_ffn_ref(x, gate_w, w1, w2, w3):
        import jax, jax.numpy as jnp
        import numpy as np
        NUM_ACT = 2
        B, S, D = x.shape
        xt = x.reshape(-1, D)
        scores = jnp.einsum('ti,ei->te', xt, gate_w)
        probs = jax.nn.softmax(scores, axis=-1)
        expert_weights, expert_indices = jax.lax.top_k(probs, NUM_ACT)
        expert_weights = expert_weights / expert_weights.sum(axis=-1, keepdims=True)
        x1 = jax.nn.silu(jnp.einsum('ti,eoi->teo', xt, w1))
        x3 = jnp.einsum('ti,eoi->teo', xt, w3)
        expert_outs_all = jnp.einsum('teo,eio->tei', x1 * x3, w2)
        sel = jnp.take_along_axis(expert_outs_all, expert_indices[:, :, None], axis=1)
        out = jnp.einsum('tai,ta->ti', sel, expert_weights)
        return out.reshape(B, S, D)
    x = L0_attn_x
    xn = _layernorm(x, axis=-1)
    s = _L0_attn_ref(xn, L0_attn_Wqkv, L0_attn_Wout)
    g = _silu(_L0_ffn_ref(xn, L0_ffn_gate_w, L0_ffn_w1, L0_ffn_w2, L0_ffn_w3))
    x = x + s * g
    return x

_drawn_inputs = setup_inputs


def setup_inputs(seed=0):
    import zlib

    import numpy as np

    out = dict(_drawn_inputs(seed))
    spreads = {}
    factors = {'L0_attn_Wqkv': 8.0,
     'L0_attn_Wout': 8.0,
     'L0_ffn_gate_w': 8.0,
     'L0_ffn_w1': 8.0,
     'L0_ffn_w2': 8.0,
     'L0_ffn_w3': 8.0}
    for name, (base, spread) in spreads.items():
        noise = np.random.default_rng([zlib.crc32(name.encode()), seed]).standard_normal(out[name].shape)
        drawn = base * np.exp(spread * noise) if base else spread * noise
        out[name] = jnp.asarray(drawn.astype(out[name].dtype))
    for name, factor in factors.items():
        out[name] = (out[name] * factor).astype(out[name].dtype)
    return out
```

```python
import concourse.bass as bass
from concourse import mybir
from contextlib import ExitStack
import numpy as np

F32 = mybir.dt.float32
F16 = mybir.dt.float16
BF16 = mybir.dt.bfloat16
I32 = mybir.dt.int32
U32 = mybir.dt.uint32
ALU = mybir.AluOpType
ACT = mybir.ActivationFunctionType
AX = mybir.AxisListType.X
ABSMAX = bass.bass_isa.ReduceOp.absmax

P = 128
B, S, D = 4, 1024, 256
T = B * S
NT = T // P
H = 16
HD = D // H
E = 8
NI = 512
QG = 3 * D + E
CLEARED = 10


class Count:
    STRIDE = 4

    def __init__(self, loop, at):
        self.loop, self.at = loop, at

    def __sub__(self, k):
        return type(self)(self.loop, self.at - k)

    def times(self, k, plus=0):
        return self.share(1, k, plus)

    def share(self, n, k, plus=0):
        rest = self.at // n * k + plus
        return rest if self.loop is None else self.loop * (self.STRIDE // n * k) + rest

    def quarters(self, k, plus=0):
        return self.share(4, k, plus)

    def eighths(self, k, plus=0):
        return self.share(8, k, plus)


class Eighth(Count):
    STRIDE = 8


def project(nc, bank, x, wqg, rope_cos, rope_sin, ident_h, ident32_h, masks_h, qT_d, kT_d, v_d, ident, ident_f, masks, xall, xhl, logits, pow2, xg_d, ranks_h, small_h, rank_f, small):
    with ExitStack() as ctx:
        def sb(name, shape, dt):
            return ctx.enter_context(nc.sbuf_tensor(name, shape, dt))

        def sem(name):
            return ctx.enter_context(nc.semaphore(name))

        wqg_f = sb("wqg_f", [P, 2, QG], F32)
        wqg_h = sb("wqg_h", [P, 2, QG], F16)
        wqg_l = sb("wqg_l", [P, 2, QG], F16)
        cos_sb = sb("cos_sb", [P, NT, HD], F32)
        sin_sb = sb("sin_sb", [P, NT, HD], F32)
        masks_f = sb("masks_f", [P, 3, P], F32)
        amax = sb("amax", [P, 2], F32)
        amax_all = sb("amax_all", [P, 2], F32)
        rscale = sb("rscale", [P, 2], F32)
        stats = sb("stats", [P, NT, 6], F32)
        mv = sb("mv", [P, NT, 2], F32)
        rstd = sb("rstd", [P, 4, NT], F32)
        zeros = sb("zeros", [P, 1, 2 * D], F16)
        eps = sb("eps", [P, 1], F32)
        xn = sb("xn", [P, 2, D], F32)
        xT = sb("xT", [P, 2, 4, P], F16)
        ra = sb("ra", [P, 2, 512], F32)
        rb = sb("rb", [P, 2, 512], F32)
        qk = sb("qk", [P, 4, 512], F32)
        qaug = sb("qaug", [P, 2, H, 4, HD], F16)
        kaug = sb("kaug", [P, 2, H, 4, HD], F16)
        vaug = sb("vaug", [P, 4, H, 32], F32)
        qst = sb("qst", [P, 2, 8, 2 * P], F16)
        kst = sb("kst", [P, 2, 8, 2 * P], F16)

        names = """const_in w_in x_in0 x_in1 x_in2 x_in3 amax_done amax_sum weight_done set_done v_zero bn_stats bn_aggr std rstd
                   xn_done hi_done lo_done xtr_done xT_done qkv_done rope_done qk_done v_done lg_done qk_hi qk_lo aug_done q_evac k_evac
                   q_out0 q_out1 k_out0 k_out1 v_out0 v_out1 v_out2 v_out3 sp_passed zero_set zero_out late_in""".split()
        s = {n: sem(n) for n in names}

        ps_x = [bank[0], bank[1]]
        ps_qk = [bank[2], bank[3]]
        ps_vg = [bank[4], bank[5]]
        ps_tq, ps_tk = bank[6], bank[7]
        TURN, PRODUCT, ROPE, HALVES, REST, STORE = 1, 2, 3, 4, 5, 6
        PEELED = 8

        def pipeline(eng, step):
            for n in range(PEELED):
                step(Count(None, n), n % 4)
            with eng.Fori(0, (NT - PEELED) // 4) as i:
                for u in range(4):
                    step(Count(i, PEELED + u), u)
            for n in range(NT, NT + STORE):
                step(Count(None, n), n % 4)

        def live(n):
            return n.loop is not None or 0 <= n.at < NT

        def after(eng, signal, n):
            if not isinstance(n, int) or n > 0:
                eng.wait_ge(signal, n)

        block = ctx.enter_context(nc.Block())

        @block.sync
        def _(sp):
            for n in ("q_out0", "q_out1", "k_out0", "k_out1"):
                sp.sem_inc(s[n], 16)
            sp.dma_start(wqg_f[:], wqg.rearrange("(c p) n -> p c n", p=P)).then_inc(s["w_in"], 16)
            for c in range(4):
                r = NT // 4
                sp.dma_start(xall[:, c * r:(c + 1) * r, :], x[c * r * P:(c + 1) * r * P, :].rearrange("(t p) d -> p t d", p=P)).then_inc(s["x_in%d" % c], 16)
            sp.dma_start(ident[:], ident_h).then_inc(s["const_in"], 16)
            sp.dma_start(ident_f[:], ident32_h).then_inc(s["const_in"], 16)
            sp.dma_start(masks_f[:], masks_h).then_inc(s["const_in"], 16)
            sp.dma_start(cos_sb[:], rope_cos.rearrange("(t p) d -> p t d", p=P)).then_inc(s["const_in"], 16)
            sp.dma_start(sin_sb[:], rope_sin.rearrange("(t p) d -> p t d", p=P)).then_inc(s["const_in"], 16)

            sp.dma_start(rank_f[:], ranks_h).then_inc(s["late_in"], 16)
            sp.dma_start(small[:], small_h).then_inc(s["late_in"], 16)
            sp.wait_ge(s["zero_set"], 1)

            def passed(n):
                if n.loop is not None:
                    sp.sem_inc(s["sp_passed"], 1)

            def step(n, u):
                tv, tq = n - ROPE, n - STORE
                row, pair, clear = tv.times(P), (tq - 1).times(P), n.quarters(CLEARED * P)
                if n.loop is not None:
                    row, pair, clear = sp.snap(row), sp.snap(pair), sp.snap(clear)
                if live(n) and u == 3:
                    sp.dma_start(xg_d[bass.ds(clear, CLEARED * P), :].rearrange("(p r) c -> p r c", r=CLEARED),
                                 zeros[:].broadcast_to([P, CLEARED, 2 * D])).then_inc(s["zero_out"], 16)
                if live(tv):
                    v = (u - ROPE) % 4
                    sp.wait_ge(s["v_done"], tv.times(1, 1))
                    passed(tv)
                    sp.dma_start(v_d[bass.ds(row, P), :], vaug[:, v].rearrange("p h d -> p (h d)")).then_inc(s["v_out%d" % v], 16)
                v = (u - STORE) % 4
                if live(tq) and v % 2:
                    sp.wait_ge(s["q_evac"], tq.times(1, 1))
                    passed(tq)
                    sp.dma_start(qT_d[:, :, bass.ds(pair, 2 * P)].rearrange("h p t -> p h t"), qst[:, v // 2]).then_inc(s["q_out%d" % (v // 2)], 16)
                    sp.wait_ge(s["k_evac"], tq.times(1, 1))
                    passed(tq)
                    sp.dma_start(kT_d[:, :, bass.ds(pair, 2 * P)].rearrange("h p t -> p h t"), kst[:, v // 2]).then_inc(s["k_out%d" % (v // 2)], 16)
            pipeline(sp, step)
            sp.wait_ge(s["late_in"], 32)
            sp.wait_ge(s["zero_out"], 16 * (NT // 4))
            for n in range(4):
                sp.wait_ge(s["v_out%d" % n], 4 * NT)
            for n in range(2):
                sp.wait_ge(s["q_out%d" % n], 4 * NT + 16)
                sp.wait_ge(s["k_out%d" % n], 4 * NT + 16)

        @block.gpsimd
        def _(pool):
            pool.memset(zeros[:], 0.0).then_inc(s["zero_set"], 1)
            pool.memset(eps[:], 1e-5).then_inc(s["set_done"], 1)
            pool.memset(qaug[:, :, :, 3, :], 0.0).then_inc(s["set_done"], 1)
            pool.memset(kaug[:, :, :, 3, 2:HD], 0.0).then_inc(s["set_done"], 1)
            pool.memset(kaug[:, :, :, 3, 0:2], 32768.0).then_inc(s["set_done"], 1)
            pool.memset(vaug[:, :, :, HD:32], 0.0).then_inc(s["v_zero"], 1)
            pool.wait_ge(s["v_zero"], 1)
            pool.memset(vaug[:, :, :, HD], 1.0).then_inc(s["set_done"], 1)
            pool.wait_ge(s["amax_done"], 2)
            pool.partition_all_reduce(amax_all[:], amax[:], P, ABSMAX).then_inc(s["amax_sum"], 1)

            def step(n, u):
                t, b, v = n - ROPE, (u - ROPE) % 2, (u - ROPE) % 4
                if live(t):
                    pool.wait_ge(s["rope_done"], t.times(2, 2))
                    after(pool, s["qk_lo"], t.times(2, -6))
                    pool.tensor_tensor(qk[:, v], ra[:, b], rb[:, b], ALU.add).then_inc(s["qk_done"], 1)
                if live(n):
                    pool.wait_ge(s["hi_done"], n.times(1, 1))
                    pool.tensor_tensor(xhl[:, n.times(1), D:2 * D], xn[:, u % 2], xhl[:, n.times(1), 0:D], ALU.subtract).then_inc(s["lo_done"], 1)
            pipeline(pool, step)

        @block.scalar
        def _(act):
            act.wait_ge(s["set_done"], 5)
            act.wait_ge(s["bn_aggr"], NT)
            act.activation(rstd[:, 0], mv[:, :, 1], ACT.Sqrt, bias=eps[:, 0:1]).then_inc(s["std"], 1)

            def step(n, u):
                t, b = n - PRODUCT, (u - PRODUCT) % 2
                if live(t):
                    act.wait_ge(s["xtr_done"], t.times(1, 1))
                    after(act, s["qkv_done"], t.times(1, -1))
                    act.activation(xT[:, b].rearrange("p c t -> p (c t)"), ps_x[b][:, 0:256].bitcast(F16), ACT.Copy).then_inc(s["xT_done"], 1)
                t, b, v = n - ROPE, (u - ROPE) % 2, (u - ROPE) % 4
                if live(t):
                    act.wait_ge(s["qkv_done"], t.times(1, 1))
                    after(act, s["v_out%d" % v], t.quarters(16))
                    act.activation(vaug[:, v, :, 0:HD], ps_vg[b][:, 0:D].rearrange("p (h d) -> p h d", d=HD), ACT.Copy).then_inc(s["v_done"], 1)
                    act.activation(logits[:, t.times(1), :], ps_vg[b][:, D:D + E], ACT.Copy).then_inc(s["lg_done"], 1)
                t, c, h = n - STORE, ((u - STORE) % 4) // 2, ((u - STORE) % 2) * P
                if live(t):
                    act.wait_ge(s["aug_done"], t.times(1, 1))
                    act.wait_ge(s["q_out%d" % c], t.quarters(16, 16))
                    act.activation(qst[:, c, :, h:h + P], ps_tq[:].bitcast(F16).rearrange("p (h t) -> p h t", h=8), ACT.Copy).then_inc(s["q_evac"], 1)
                t, b, v = n - HALVES, (u - HALVES) % 2, (u - HALVES) % 4
                if live(t):
                    act.wait_ge(s["qk_done"], t.times(1, 1))
                    after(act, s["aug_done"], t.times(1, -1))
                    q3 = qk[:, v, 0:D].rearrange("p (h o d) -> p h o d", o=1, d=HD).broadcast_to([P, H, 2, HD])
                    k3 = qk[:, v, D:2 * D].rearrange("p (h o d) -> p h o d", o=1, d=HD).broadcast_to([P, H, 2, HD])
                    act.activation(qaug[:, b, :, 0:2, :], q3, ACT.Copy).then_inc(s["qk_hi"], 1)
                    act.activation(kaug[:, b, :, 0:3:2, :], k3, ACT.Copy).then_inc(s["qk_hi"], 1)
                if live(n):
                    act.wait_ge(s["xn_done"], n.times(1, 1))
                    act.activation(xhl[:, n.times(1), 0:D], xn[:, u % 2], ACT.Copy).then_inc(s["hi_done"], 1)
            pipeline(act, step)

        @block.vector
        def _(dve):
            dve.wait_ge(s["w_in"], 16)
            dve.tensor_reduce(amax[:, 0:1], wqg_f[:, :, 0:3 * D], mybir.AxisListType.XY, ALU.max, apply_absolute_value=True).then_inc(s["amax_done"], 1)
            dve.tensor_reduce(amax[:, 1:2], wqg_f[:, :, 3 * D:QG], mybir.AxisListType.XY, ALU.max, apply_absolute_value=True).then_inc(s["amax_done"], 1)

            def statistics(a, z):
                for t in range(a, z):
                    dve.wait_ge(s["x_in%d" % (t * 4 // NT)], 16)
                    dve.bn_stats(stats[:, t], xall[:, t]).then_inc(s["bn_stats"], 1)
            statistics(0, 8)
            dve.wait_ge(s["amax_sum"], 1)
            dve.tensor_scalar(rscale[:], amax_all[:], 2.0 ** -100, None, ALU.max).then_inc(s["weight_done"], 1)
            dve.wait_ge(s["weight_done"], 1)
            dve.tensor_scalar(pow2[:].bitcast(U32), rscale[:].bitcast(U32), 0x7F800000, None, ALU.bitwise_and).then_inc(s["weight_done"], 1)
            dve.wait_ge(s["weight_done"], 2)
            dve.reciprocal(rscale[:], pow2[:]).then_inc(s["weight_done"], 1)
            dve.wait_ge(s["weight_done"], 3)
            dve.tensor_scalar(rscale[:], rscale[:], 2.0 ** 14, None, ALU.mult).then_inc(s["weight_done"], 1)
            dve.wait_ge(s["weight_done"], 4)
            for n, (a, z) in enumerate(((0, 3 * D), (3 * D, QG))):
                dve.tensor_scalar(wqg_h[:, :, a:z], wqg_f[:, :, a:z], rscale[:, n:n + 1], None, ALU.mult).then_inc(s["weight_done"], 1)
            dve.wait_ge(s["weight_done"], 6)
            for n, (a, z) in enumerate(((0, 3 * D), (3 * D, QG))):
                dve.scalar_tensor_tensor(out=wqg_l[:, :, a:z], in0=wqg_f[:, :, a:z], scalar=rscale[:, n:n + 1], in1=wqg_h[:, :, a:z],
                                         op0=ALU.mult, op1=ALU.subtract).then_inc(s["weight_done"], 1)
            statistics(8, NT)
            dve.wait_ge(s["const_in"], 80)
            dve.tensor_copy(masks[:], masks_f[:])
            for t in range(NT):
                dve.wait_ge(s["bn_stats"], t + 1)
                dve.bn_aggr(mv[:, t], stats[:, t]).then_inc(s["bn_aggr"], 1)
            dve.wait_ge(s["std"], 1)
            dve.reciprocal(rstd[:, 1], rstd[:, 0]).then_inc(s["rstd"], 1)
            dve.wait_ge(s["rstd"], 1)
            dve.tensor_tensor(rstd[:, 2], rstd[:, 1], rstd[:, 1], ALU.mult).then_inc(s["rstd"], 1)
            dve.wait_ge(s["rstd"], 2)
            dve.scalar_tensor_tensor(out=rstd[:, 3], in0=mv[:, :, 1], scalar=1e-5, in1=rstd[:, 2], op0=ALU.add, op1=ALU.mult).then_inc(s["rstd"], 1)
            dve.wait_ge(s["rstd"], 3)
            dve.tensor_scalar(rstd[:, 2], rstd[:, 3], -0.5 * 2048, 1.5 * 2048, ALU.mult, ALU.add).then_inc(s["rstd"], 1)
            dve.wait_ge(s["rstd"], 4)
            dve.tensor_tensor(rstd[:, 0], rstd[:, 1], rstd[:, 2], ALU.mult).then_inc(s["rstd"], 1)
            dve.wait_ge(s["rstd"], 5)

            def step(n, u):
                if live(n):
                    after(dve, s["lo_done"], n.times(1, -1))
                    dve.tensor_scalar(xn[:, u % 2], xall[:, n.times(1)], mv[:, n.times(1), 0:1], rstd[:, 0, bass.ds(n.times(1), 1)], ALU.subtract, ALU.mult).then_inc(s["xn_done"], 1)
                t, b, v = n - REST, (u - REST) % 2, (u - REST) % 4
                if live(t):
                    dve.wait_ge(s["qk_hi"], t.times(2, 2))
                    for (aug, part, o) in ((qaug, 2, 0), (kaug, 1, D)):
                        dve.tensor_tensor(aug[:, b, :, part, :], qk[:, v, o:o + D].rearrange("p (h d) -> p h d", d=HD), aug[:, b, :, 0, :],
                                          ALU.subtract).then_inc(s["qk_lo"], 1)
                t, b = n - ROPE, (u - ROPE) % 2
                if live(t):
                    dve.wait_ge(s["qkv_done"], t.times(1, 1))
                    after(dve, s["qk_done"], t.times(1, -1))
                    src = ps_qk[b][:].rearrange("p (h d) -> p h d", d=HD)
                    cs = cos_sb[:, t.times(1), :].rearrange("p (o d) -> p o d", o=1).broadcast_to([P, 2 * H, HD])
                    dve.tensor_tensor(ra[:, b].rearrange("p (h d) -> p h d", d=HD), src, cs, ALU.mult).then_inc(s["rope_done"], 1)
                    sn = sin_sb[:, t.times(1), :].rearrange("p (o d e) -> p o d e", o=1, e=2).broadcast_to([P, 2 * H, HD // 2, 2])
                    rot = ps_qk[b][:].rearrange("p (h d e) -> p h d e", d=HD // 2, e=2)[:, :, :, ::-1]
                    dve.tensor_tensor(rb[:, b].rearrange("p (h d e) -> p h d e", d=HD // 2, e=2), rot, sn, ALU.mult).then_inc(s["rope_done"], 1)
                t, c, h = n - STORE, ((u - STORE) % 4) // 2, ((u - STORE) % 2) * P
                if live(t):
                    dve.wait_ge(s["aug_done"], t.times(1, 1))
                    dve.wait_ge(s["k_out%d" % c], t.quarters(16, 16))
                    dve.tensor_copy(kst[:, c, :, h:h + P], ps_tk[:].bitcast(F16).rearrange("p (h t) -> p h t", h=8)).then_inc(s["k_evac"], 1)
            pipeline(dve, step)

        @block.tensor
        def _(pe):
            pe.wait_ge(s["weight_done"], 8)
            pe.wait_ge(s["const_in"], 80)

            def step(n, u):
                t, b = n - TURN, (u - TURN) % 2
                if live(t):
                    pe.wait_ge(s["lo_done"], t.times(1, 1))
                    after(pe, s["xT_done"], t.times(1, -1))
                    for c in range(4):
                        m = pe.matmul(ps_x[b][:, 0:256].bitcast(F16)[:, c * P:(c + 1) * P], xhl[:, t.times(1), c * P:(c + 1) * P], ident[:],
                                      is_transpose=True, start=True, stop=True)
                    m.then_inc(s["xtr_done"], 1)
                t, b = n - PRODUCT, (u - PRODUCT) % 2
                if live(t):
                    pe.wait_ge(s["xT_done"], t.times(1, 1))
                    after(pe, s["rope_done"], t.times(2, -2))
                    after(pe, s["lg_done"], t.times(1, -1))
                    terms = [(0, wqg_h), (0, wqg_l), (2, wqg_h)]
                    for k in range(2):
                        for m_, (xo, w) in enumerate(terms):
                            first, last = k == 0 and m_ == 0, k == 1 and m_ == 2
                            pe.matmul(ps_qk[b][:], xT[:, b, xo + k], w[:, k, 0:512], start=first, stop=last)
                            m = pe.matmul(ps_vg[b][:, 0:QG - 512], xT[:, b, xo + k], w[:, k, 512:QG], start=first, stop=last)
                    m.then_inc(s["qkv_done"], 1)
                t, b = n - REST, (u - REST) % 2
                if live(t):
                    pe.wait_ge(s["qk_lo"], t.times(2, 2))
                    after(pe, s["q_evac"], t.times(1))
                    after(pe, s["k_evac"], t.times(1))
                    for aug, ps in ((qaug, ps_tq), (kaug, ps_tk)):
                        for c in range(8):
                            m = pe.matmul(ps[:].bitcast(F16)[:, c * P:(c + 1) * P], aug[:, b, 2 * c:2 * c + 2].rearrange("p h e d -> p (h e d)"), ident[:],
                                          is_transpose=True, start=True, stop=True)
                    m.then_inc(s["aug_done"], 1)
            pipeline(pe, step)


GROUPS = 16
GH = 4
NB = S // P


class Group:

    def __init__(self, loop, at):
        self.loop, self.at = loop, at

    def __add__(self, k):
        return Group(self.loop, self.at + k)

    def times(self, k, plus=0):
        return self.at * k + plus if self.loop is None else self.loop * (3 * k) + (self.at * k + plus)

    def thirds(self, k, plus=0):
        n = self.at // 3 * k + plus
        return n if self.loop is None else self.loop * k + n


class Matrix:

    def __init__(self, loop, each, at):
        self.loop, self.each, self.at = loop, each, at
        self.kind, self.splits = at % 3, at >= 3 * E

    def __add__(self, k):
        return Matrix(self.loop, self.each, self.at + k)

    def times(self, k, plus=0):
        return self.at * k + plus if self.loop is None else self.loop * (self.each * k) + (self.at * k + plus)

    def turns(self, k, plus=0):
        n = self.at // 3 * k + plus
        return n if self.loop is None else self.loop * (self.each // 3 * k) + n

    def expert(self, eng):
        n = self.at // 3 % E
        return n if self.loop is None else eng.snap((self.loop * (self.each // 3) + self.at // 3) % E)


SLOTS_OF = {4: (6, 16, 26, 36), 2: (10, 28), 3: (8, 20, 32)}


def width_units():
    units = []
    for j in range(NB):
        w = S - P * j
        if w > 512:
            units += [(j, [h], c, w // 2) for h in range(GH) for c in (0, w // 2)]
        else:
            per = max(1, 512 // w) if w != 384 else 1
            units += [(j, list(range(h, h + per)), 0, w) for h in range(0, GH, per)]
    return units


UNITS = width_units()
NU = len(UNITS)
LEAD = 10
RING = 6


def pieces(j):
    cuts = [c for c in (256, 512, 768) if c - P * j > P and (j > 0 or c == 512)] + [S]
    return list(zip([P * j] + cuts[:-1], cuts))


def order(next_max, after_next):
    then = {1: (NB - 2, 0), 3: (NB - 1, 0), 12: (0, 0), 14: (0, 1), 17: (1, 0), 19: (1, 1), 21: (1, 2), 25: (2, 0), 27: (2, 1), 29: (2, 2),
            33: (3, 0), 34: (3, 1), 37: (4, 0), 38: (4, 1), 41: (5, 0)}
    assert sorted(then.values()) == [(j, p) for j in range(NB) for p in range(len(pieces(j)))]
    seq = []
    for k in range(NU):
        seq.append(("S", k, 0))
        if k == 35:
            seq.append(("T", 0, 1))
        if k == 8:
            seq.append(("O", 0, 0))
        seq += [("V", *then[k])] if k in then else []
        seq.append(("M", k + LEAD, 1) if k + LEAD < NU else ("M", k + LEAD - NU, 2))
    slots, n = {}, 0
    for e in seq:
        if e[0] in "MST":
            slots[e[:2]] = n % RING
            n += 1
    seq = [e for e in seq if e[0] not in "MT" or (next_max if e[2] == 1 else after_next)]
    return seq, slots


def last_unit(j):
    return max(n for n in range(NU) if UNITS[n][0] == j)


assert NU == 43
SEQ, SLOT = order(True, True)
BEFORE_LAST_SEQ, _ = order(True, False)
LAST_SEQ, _ = order(False, False)


def previous(seq, before, at):
    slot = SLOT[seq[at][:2]]
    for back, events in ((0, seq[:at]), (1, before)):
        for f in reversed(events):
            if f[0] in "MST" and SLOT[f[:2]] == slot:
                return f, back


NBLK = 39
SLOT_BLOCK = 2 * P
SLOTS = NBLK * SLOT_BLOCK
WCOLS = 3 * 1024
BOTH_AT = 12
EXP_AT = 14
ALL_SCALES = 9
ROUTED = 14 + 3 + 1 + 8 + 1 + 6 + 2 + 6


def attention(nc, psum, qT_d, kT_d, v_d, o_d, ident, ident_f, masks, pow2, w_all, xg_d, wts, escale, xhl, logits, rank_f, small, gates, slot_of, expert_of):
    with ExitStack() as ctx:
        def sb(name, shape, dt):
            return ctx.enter_context(nc.sbuf_tensor(name, shape, dt))

        def sem(name):
            return ctx.enter_context(nc.semaphore("at_" + name))

        kT = [sb(f"kT{n}", [P, 2, S], F16) for n in range(3)]
        qz = [sb(f"qz{n}", [P, GH, S], F16) for n in range(3)]
        vt = [sb(f"vt{n}", [P, NB, GH, 32], F32) for n in range(3)]
        probs = [sb(f"probs{n}", [P, GH, S - n * P], F32) for n in range(2)]
        row_max = sb("row_max", [P, 2, GH, NB], F32)
        neg_max = sb("neg_max", [P, P], F16)
        max_rows = sb("max_rows", [2 * GH * NB, P], F16)
        oT = sb("oT", [P, S], F32)
        den = sb("den", [P, NB, GH], F32)
        den2 = sb("den2", [P, NB, GH], F32)
        osb_all = sb("osb", [P, 3, NB, GH * HD], F32)
        osb = [osb_all[:, n] for n in range(3)]
        work = osb_all[:].rearrange("p n b d -> p (n b d)")
        sel = work[:, 0:4 * NT * E].rearrange("p (k t e) -> p k t e", k=4, t=NT)
        cnt = work[:, 4 * NT * E:5 * NT * E].rearrange("p (e t) -> p e t", e=E)

        load = [sem(f"load{n}") for n in range(3)]
        rows_in = [sem(f"rows_in{n}") for n in range(3)]
        o_out = [sem(f"o_out{n}") for n in range(3)]
        zeroed, m_ready, m_taken, s_ready, s_taken, v_done, neg1, neg2, turned, rows_copied, o_copied, o_turned, den_done, o_done, passed_, primed = (
            sem(n) for n in "zeroed m_ready m_taken s_ready s_taken v_done neg1 neg2 turned rows_copied o_copied o_turned den_done o_done passed primed".split())

        stage = sb("stage", [P, 3, 1024], F32)
        amax_w = sb("amax_w", [P, 3, E], F32)
        amax_k = sb("amax_k", [P, 2, 3], F32)
        pow2w = sb("pow2w", [P, 3], F32)
        rs = sb("rs", [P, 3], F32)
        rank_w = sb("rank_w", [P, 2, P], BF16)
        m = sb("m", [P, 8, NT], F32)
        both = sb("both", [P, NT, E], BF16)
        sones = sb("sones", [P, NBLK], F32)
        ex = sb("ex", [P, 4, E], F32)
        nbi = sb("nbi", [P, 2, E], I32)
        gef = sb("gef", [P, 2, NBLK], F32)
        gsc = sb("gsc", [P, 1], F32)
        stage_in = [sem(f"stage_in{n}") for n in range(3)]
        whole_max, ew_max, ew_all, ew_sum, ones_set, step_, ranked, exped, scattered, w_hi, w_lo, act_passed = (sem(n) for n in "whole_max ew_max ew_all ew_sum ones_set route ranked exped scattered w_hi w_lo act_passed".split())

        bank = [psum[:, n, :] for n in range(8)]
        pv_view = psum[:, 6:8, :].rearrange("p b c -> p (b c)")
        ones = sb("ones", [P, 512], BF16)
        scales = sb("scales", [P, 3], F32)
        score_scale, value_scale = scales[:, 1:2], scales[:, 2:3]
        mask_l, mask_r = masks[:, 0], masks[:, 1:3]
        scaled = sem("scaled")

        def place(h):
            return h % 2 * 2 + h // 2

        pv = (bank[6], bank[7])

        def unit_view(slot, heads, w):
            return bank[slot][:, 0:len(heads) * w].rearrange("p (h w) -> p h w", w=w)

        block = ctx.enter_context(nc.Block())

        def walk(eng, step, between=lambda: None):
            with eng.Fori(0, 2) as i:
                for u in range(3):
                    step(Group(i, u), u, True, True, [Matrix(i, 12, 4 * u + n) for n in range(4)])
            between()
            with eng.Fori(0, 2) as i:
                for u in range(3):
                    step(Group(i, 6 + u), u, True, True, [Matrix(i, 6, 3 * E + 2 * u + n) for n in range(2)])
            for n in range(12, GROUPS):
                step(Group(None, n), n % 3, n + 1 < GROUPS, n + 2 < GROUPS, [Matrix(None, 0, 3 * E + 12 + 3 * (n - 12) + k) for k in range(3)])

        @block.sync
        def _(sp):
            def fetch(g, u):
                if g.loop is None:
                    b, pair = g.at // 4, g.at % 4 * 2
                else:
                    n = sp.snap(g.times(1))
                    b, pair = sp.snap(n // 4), sp.snap(n % 4 * 2)
                return b, pair

            def start(b, pair, u):
                cols = bass.ds(b * S, S)
                sp.dma_start(kT[u][:], kT_d[bass.ds(pair, 2), :, cols].rearrange("r p t -> p r t")).then_inc(load[u], 16)
                for k in range(2):
                    sp.dma_start(qz[u][64 * k:64 * k + 64, 2 * k:2 * k + 2, :],
                                 qT_d[bass.ds(pair, 2), 64 * k:64 * k + 64, cols].rearrange("r p t -> p r t")).then_inc(load[u], 16)
                sp.dma_start(vt[u][:], v_d[cols, bass.ds(pair * 64, GH * 32)].rearrange("(n p) d -> p n (d)", p=P)).then_inc(load[u], 16)

            def rows(g, u):
                for k in range(2):
                    for part in range(2):
                        r, n = 48 + 64 * k + part, (2 * k + part) * 2 * NB
                        sp.dma_start(qz[u][r:r + 1, 2 * k:2 * k + 2, :], max_rows[n:n + 2 * NB, :]).then_inc(rows_in[u], 16)

            def passed(g):
                if g.loop is not None:
                    sp.sem_inc(passed_, 1)
            for n in range(3):
                b, pair = fetch(Group(None, n), n)
                start(b, pair, n)
            for n in range(3):
                sp.sem_inc(o_out[n], 32 if n == 2 else 16)
            sp.wait_ge(rows_copied, 1)
            rows(Group(None, 0), 0)

            def step(g, u):
                ahead = live_fetch = None
                if g.loop is not None or g.at + 3 < GROUPS:
                    ahead = fetch(g + 3, u)
                if g.loop is not None or g.at >= 1:
                    prev = fetch(g + (-1), u)
                if g.loop is not None or g.at + 1 < GROUPS:
                    sp.wait_ge(rows_copied, g.times(1, 2))
                    passed(g)
                    rows(g + 1, (u + 1) % 3)
                if g.loop is not None or g.at >= 1:
                    sp.wait_ge(o_done, g.times(1, 1))
                    passed(g)
                    store(prev, (u - 1) % 3)
                if ahead is not None:
                    sp.wait_ge(v_done, g.times(NB, 2 * NB))
                    passed(g)
                    start(*ahead, u)

            def store(at, u):
                b, pair = at
                sp.dma_start(o_d[bass.ds(b * S, S), bass.ds(pair * 2 * HD, GH * HD)].rearrange("(n p) d -> p n d", p=P), osb[u]).then_inc(o_out[u], 16)
            step(Group(None, 0), 0)
            with sp.Fori(0, 4) as i:
                for u in (1, 2, 3):
                    step(Group(i, u), u % 3)
            for n in (13, 14, 15):
                step(Group(None, n), n % 3)
            sp.wait_ge(o_done, GROUPS + 1)
            store(fetch(Group(None, 15), 0), 0)
            sp.wait_ge(o_out[0], 16 * 7)
            sp.wait_ge(o_out[1], 16 * 6)
            sp.wait_ge(o_out[2], 16 * 7)

        @block.gpsimd
        def _(pool):
            pool.memset(ones[:], 1.0).then_inc(zeroed, 1)
            pool.memset(row_max[:, 1], -3e38).then_inc(ones_set, 1)
            pool.memset(sones[:], 1.0).then_inc(ones_set, 1)
            pool.tensor_copy(rank_w[:], rank_f[:]).then_inc(ones_set, 1)
            pool.memset(neg_max[:, P // 2:P], 0.0).then_inc(zeroed, 1)
            for n in range(3):
                for k in range(2):
                    pool.wait_ge(zeroed, 2 + 2 * n + k)
                    pool.memset(qz[n][64 - 64 * k:128 - 64 * k, 2 * k:2 * k + 2, :], 0.0).then_inc(zeroed, 1)
            pool.memset(probs[0][:, :, 0:2 * P], 0.0).then_inc(zeroed, 1)
            pool.memset(probs[1][:, :, 0:P], 0.0).then_inc(zeroed, 1)
            pool.wait_ge(step_, ROUTED)
            for t in range(NT):
                for k in range(2):
                    pool.indirect_dma_start(out=xg_d, out_offset=bass.IndirectOffsetOnAxis(ap=slot_of[:, k, t:t + 1], axis=0),
                                            in_=xhl[:, t, :], in_offset=None).then_inc(scattered, 16)
            pool.wait_ge(scattered, 16 * 2 * NT)
            pool.wait_ge(ew_all, 1)
            pool.partition_all_reduce(amax_k[:, 1], amax_k[:, 0], P, ABSMAX).then_inc(ew_sum, 1)

        @block.scalar
        def _(act):
            act.wait_ge(step_, EXP_AT)
            act.activation(m[:, 5], m[:, 4], ACT.Exp, scale=gsc[:]).then_inc(exped, 1)
            act.sem_inc(s_taken, NU)
            act.wait_ge(scaled, 3)

            def take_outputs(g, n):
                act.wait_ge(v_done, n)
                act.activation(oT[:], pv_view, ACT.Copy).then_inc(o_copied, 1)

            def load_stage(m):
                kind, c = m.kind, 4 if m.kind == 2 else 2
                if m.loop is not None:
                    act.sem_inc(act_passed, 1)
                act.dma_start(stage[:, kind].rearrange("p (c n) -> p c n", c=c),
                              wts[kind][bass.ds(m.expert(act), 1)].rearrange("e (c p) n -> p (e c) n", p=P)).then_inc(stage_in[kind], 16)

            def matrix(m):
                act.wait_ge(w_lo if m.splits else ew_max, m.times(1, 1 - (3 * E if m.splits else 0)))
                if m.loop is not None or m.at + 2 < 6 * E:
                    load_stage(m + 2)
                if m.splits:
                    act.wait_ge(stage_in[m.kind], m.turns(16, 16))
                    act.activation(w_all[:, m.expert(act), 0, m.kind * 1024:(m.kind + 1) * 1024], stage[:, m.kind], ACT.Copy,
                                   scale=rs[:, m.kind:m.kind + 1]).then_inc(w_hi, 1)

            def between():
                act.wait_ge(ew_all, ALL_SCALES)
                act.wait_ge(scattered, 16 * 2 * NT)
            act.sem_inc(ew_max, 1)
            act.sem_inc(w_lo, 1)
            for n in range(2):
                load_stage(Matrix(None, 0, n))

            def step(g, u, next_max, after_next, matrices):
                for k, (j, heads, q0, w) in enumerate(UNITS):
                    if k in SLOTS_OF[len(matrices)]:
                        matrix(matrices[SLOTS_OF[len(matrices)].index(k)])
                    if k == 6:
                        take_outputs(g, g.times(NB, NB))
                    if k == 0 or UNITS[k - 1][0] != j:
                        act.wait_ge(v_done, g.times(NB, NB + j - 1))
                    act.wait_ge(s_ready, g.times(NU, k + 1))
                    act.activation(probs[j % 2][:, heads[0]:heads[-1] + 1, q0:q0 + w], unit_view(SLOT["S", k], heads, w), ACT.Exp,
                                   scale=score_scale).then_inc(s_taken, 1)
            walk(act, step, between)
            take_outputs(None, NB * (GROUPS + 1))

        @block.vector
        def _(dve):
            def maxima(k, n):
                j, heads, k0, w = UNITS[k]
                i, half = NB - 1 - j, int(k0 > 0)
                dve.wait_ge(m_ready, n)
                view = unit_view(SLOT["M", k], heads, w)
                if len(heads) == GH:
                    into, view = row_max[:, 0, :, i].rearrange("p (k j) -> p j k", k=2), view.rearrange("p (j k) w -> p j k w", k=2)
                else:
                    into = row_max[:, half, place(heads[0]):place(heads[-1]) + 1:2, i]
                dve.tensor_reduce(into, view, AX, ALU.max).then_inc(m_taken, 1)

            def negate(n, last):
                dve.wait_ge(m_taken, last)
                dve.tensor_tensor(row_max[:, 0], row_max[:, 0], row_max[:, 1], ALU.max).then_inc(whole_max, 1)
                dve.wait_ge(whole_max, n)
                parts = neg_max[:, 0:P // 2].rearrange("p (k a m) -> p a k m", k=2, a=2)
                maxs = row_max[:, 0].rearrange("p (k j) n -> p k (j n)", k=2)
                dve.tensor_scalar(parts[:, 0], maxs, -2.0 ** -15, None, ALU.mult).then_inc(neg1, 1)
                dve.wait_ge(neg1, n)
                dve.scalar_tensor_tensor(out=parts[:, 1], in0=maxs, scalar=-2.0 ** -15, in1=parts[:, 0],
                                         op0=ALU.mult, op1=ALU.subtract).then_inc(neg2, 1)
                dve.wait_ge(neg2, n)

            def copy_rows(n):
                dve.wait_ge(turned, n)
                dve.tensor_copy(max_rows[:], bank[SLOT["T", 0]][0:64, 0:64].bitcast(F16)).then_inc(rows_copied, 1)

            def normalise(u, n, stored):
                dve.wait_ge(o_turned, n)
                both = pv_view.rearrange("p (n h d) -> p n h d", n=NB, h=GH)
                dve.reciprocal(den[:], both[:, :, :, HD]).then_inc(den_done, 1)
                dve.wait_ge(den_done, n * 2 - 1 if isinstance(n, int) else n * 2 - 1)
                dve.tensor_scalar(den2[:], den[:], value_scale, None, ALU.mult).then_inc(den_done, 1)
                dve.wait_ge(den_done, n * 2)
                dve.wait_ge(o_out[u], stored)
                dve.tensor_tensor(osb[u].rearrange("p n (h d) -> p n h d", h=GH), both[:, :, :, 0:HD],
                                  den2[:].rearrange("p n (h o) -> p n h o", o=1).broadcast_to([P, NB, GH, HD]), ALU.mult).then_inc(o_done, 1)

            def matrix(m):
                if m.splits:
                    e, at = m.expert(dve), slice(m.kind * 1024, (m.kind + 1) * 1024)
                    dve.wait_ge(w_hi, m.times(1, 1 - 3 * E))
                    dve.scalar_tensor_tensor(out=w_all[:, e, 1, at], in0=stage[:, m.kind], scalar=rs[:, m.kind:m.kind + 1],
                                             in1=w_all[:, e, 0, at], op0=ALU.mult, op1=ALU.subtract).then_inc(w_lo, 1)
                else:
                    dve.wait_ge(stage_in[m.kind], m.turns(16, 16))
                    dve.tensor_reduce(amax_w[:, m.kind, bass.ds(m.expert(dve), 1)], stage[:, m.kind], AX, ALU.max,
                                      apply_absolute_value=True).then_inc(ew_max, 1)

            def largest_of_all():
                dve.wait_ge(ew_max, 3 * E + 1)
                dve.tensor_reduce(amax_k[:, 0], amax_w[:], AX, ALU.max).then_inc(ew_all, 1)

            def scale_weights():
                dve.wait_ge(ew_sum, 1)
                dve.tensor_scalar(amax_k[:, 0], amax_k[:, 1], 2.0 ** -60, None, ALU.max).then_inc(ew_all, 1)
                dve.wait_ge(ew_all, 2)
                dve.tensor_scalar(pow2w[:].bitcast(U32), amax_k[:, 0].bitcast(U32), 0x7F800000, None, ALU.bitwise_and).then_inc(ew_all, 1)
                dve.wait_ge(ew_all, 3)
                dve.reciprocal(rs[:], pow2w[:]).then_inc(ew_all, 1)
                dve.tensor_scalar(escale[:, 0:1], pow2w[:, 0:1], 2.0 ** -25, None, ALU.mult).then_inc(ew_all, 1)
                dve.tensor_scalar(escale[:, 3:4], pow2w[:, 0:1], pow2w[:, 1:2], 2.0 ** -11, ALU.mult, ALU.mult).then_inc(ew_all, 1)
                dve.wait_ge(ew_all, 6)
                dve.tensor_scalar(escale[:, 1:2], rs[:, 0:1], 2.0 ** -28, None, ALU.mult).then_inc(ew_all, 1)
                dve.tensor_scalar(escale[:, 2:3], escale[:, 3:4], pow2w[:, 2:3], None, ALU.mult).then_inc(ew_all, 1)
                dve.wait_ge(ew_all, 8)
                dve.tensor_scalar(rs[:], rs[:], 2.0 ** 14, None, ALU.mult).then_inc(ew_all, 1)

            def route():
                dve.wait_ge(ones_set, 3)
                count = [0]
                incl = sel[:, 3].rearrange('p t e -> p (t e)').rearrange('p (e t) -> p e t', e=E)
                ge = sel[:, 0:2].rearrange('p k t e -> p (k t e)')[:, 0:NBLK * E].rearrange('p (b e) -> p b e', e=E)

                def link(ins):
                    count[0] += 1
                    ins.then_inc(step_, 1)
                    dve.wait_ge(step_, count[0])

                desc = small[:, 0:E].rearrange("p (o e) -> p o e", o=1).broadcast_to([P, NT, E])

                def wide(a):
                    return a.rearrange("p (t o) -> p t o", o=1).broadcast_to([P, NT, E])
                for k in range(2):
                    lg = logits[:] if k == 0 else sel[:, 2]
                    link(dve.tensor_reduce(m[:, k], lg, AX, ALU.max))
                    link(dve.tensor_tensor(sel[:, 3], lg, wide(m[:, k]), ALU.is_equal))
                    link(dve.tensor_tensor(sel[:, 3], sel[:, 3], desc, ALU.mult))
                    link(dve.tensor_reduce(m[:, 2 + k], sel[:, 3], AX, ALU.max))
                    link(dve.tensor_tensor(sel[:, k], desc, wide(m[:, 2 + k]), ALU.is_equal))
                    if k == 0:
                        link(dve.scalar_tensor_tensor(out=sel[:, 2], in0=sel[:, 0], scalar=-1e30, in1=logits[:], op0=ALU.mult, op1=ALU.add))
                link(dve.tensor_tensor(both[:], sel[:, 0], sel[:, 1], ALU.add))
                assert count[0] == BOTH_AT
                link(dve.tensor_scalar(gsc[:], pow2[:, 1:2], 2.0 ** -25, None, ALU.mult))
                link(dve.tensor_tensor(m[:, 4], m[:, 1], m[:, 0], ALU.subtract))
                assert count[0] == EXP_AT
                dve.wait_ge(exped, 1)
                link(dve.tensor_scalar(m[:, 6], m[:, 5], 1.0, None, ALU.add))
                link(dve.reciprocal(gates[:, 0], m[:, 6]))
                link(dve.tensor_tensor(gates[:, 1], gates[:, 0], m[:, 5], ALU.mult))
                dve.wait_ge(ranked, 1)
                link(dve.tensor_copy(cnt, bank[7][:, 0:NT * E].rearrange("p (t e) -> p e t", e=E)))
                for e in range(E):
                    link(dve.tensor_tensor_scan(incl[:, e, :], sones[:, 0:NT], cnt[:, e, :], 0.0, ALU.mult, ALU.add))
                link(dve.tensor_tensor(cnt, incl, cnt, ALU.subtract))
                link(dve.tensor_scalar(nbi[:, 0], incl[:, :, NT - 1], SLOT_BLOCK - 1.0, None, ALU.add))
                link(dve.tensor_scalar(nbi[:, 1], nbi[:, 0], SLOT_BLOCK.bit_length() - 1, None, ALU.arith_shift_right))
                link(dve.tensor_copy(ex[:, 0], nbi[:, 1]))
                link(dve.tensor_tensor_scan(ex[:, 1], sones[:, 0:E], ex[:, 0], 0.0, ALU.mult, ALU.add))
                link(dve.tensor_tensor(ex[:, 2], ex[:, 1], ex[:, 0], ALU.subtract))
                link(dve.tensor_scalar(ex[:, 3], ex[:, 2], float(SLOT_BLOCK), None, ALU.mult))
                link(dve.tensor_tensor(cnt, cnt, ex[:, 3].rearrange("p (e o) -> p e o", o=1).broadcast_to([P, E, NT]), ALU.add))
                link(dve.tensor_tensor(sel[:, 2], bank[6][:, 0:NT * E].rearrange("p (t e) -> p t e", e=E), cnt.rearrange("p e t -> p t e"), ALU.add))
                for k in range(2):
                    link(dve.tensor_tensor(sel[:, 3], sel[:, k], sel[:, 2], ALU.mult))
                    link(dve.tensor_reduce(m[:, 7], sel[:, 3], AX, ALU.add))
                    link(dve.tensor_copy(slot_of[:, k], m[:, 7]))
                assert count[0] == ROUTED, count
                link(dve.tensor_tensor(ge, small[:, E:E + NBLK].rearrange("p (b o) -> p b o", o=1).broadcast_to([P, NBLK, E]),
                                       ex[:, 1].rearrange("p (o e) -> p o e", o=1).broadcast_to([P, NBLK, E]), ALU.is_ge))
                link(dve.tensor_reduce(gef[:, 0], ge, AX, ALU.add))
                link(dve.tensor_scalar(gef[:, 1], gef[:, 0], E - 1.0, None, ALU.min))
                link(dve.tensor_copy(expert_of[:], gef[:, 1]))

            dve.tensor_scalar(scales[:, 0:1], pow2[:, 0:1], 2.0 ** -8, None, ALU.mult).then_inc(scaled, 1)
            dve.wait_ge(scaled, 1)
            dve.tensor_scalar(scales[:, 1:2], scales[:, 0:1], pow2[:, 0:1], None, ALU.mult).then_inc(scaled, 1)
            dve.tensor_scalar(scales[:, 2:3], pow2[:, 0:1], 2.0 ** -25, None, ALU.mult).then_inc(scaled, 1)
            route()
            for k in range(NU):
                maxima(k, k + 1)
            negate(1, NU)
            copy_rows(1)
            for k in range(LEAD):
                maxima(k, NU + k + 1)

            def between():
                largest_of_all()
                scale_weights()

            def step(g, u, next_max, after_next, matrices):
                for k in range(LEAD, NU):
                    if next_max:
                        maxima(k, g.times(NU, NU + k + 1))
                    for n, place_ in enumerate(SLOTS_OF[len(matrices)]):
                        if k == place_ + (10 if matrices[0].splits else 5):
                            matrix(matrices[n])
                    if k == LEAD + 9:
                        normalise((u - 1) % 3, g.times(1, 1), g.thirds(16, 16))
                if next_max:
                    negate(g.times(1, 2), g.times(NU, 2 * NU))
                for k in range(LEAD):
                    if after_next:
                        maxima(k, g.times(NU, 2 * NU + k + 1))
                    if k == 1 and next_max:
                        dve.wait_ge(rows_in[u], g.thirds(64, 64))
                        copy_rows(g.times(1, 2))
            walk(dve, step, between)
            normalise(0, GROUPS + 1, 16 * 6)

        @block.tensor
        def _(pe):
            def maxima(k, b):
                j, heads, k0, w = UNITS[k]
                i, ps = NB - 1 - j, bank[SLOT["M", k]]
                masked = k0 + w == S - P * j
                for n, h in enumerate(heads):
                    m = pe.matmul(ps[:, n * w:(n + 1) * w], qz[b][:, place(h), i * P:(i + 1) * P], kT[b][:, h // 2, k0:k0 + w], start=True, stop=not masked)
                    if masked:
                        m = pe.matmul(ps[:, (n + 1) * w - P:(n + 1) * w], mask_l, mask_r[:, 0, :], start=False, stop=True)
                m.then_inc(m_ready, 1)

            def scores(k, b):
                j, heads, q0, w = UNITS[k]
                ps = bank[SLOT["S", k]]
                for n, h in enumerate(heads):
                    m = pe.matmul(ps[:, n * w:(n + 1) * w], kT[b][:, h // 2, j * P:(j + 1) * P], qz[b][:, place(h), j * P + q0:j * P + q0 + w],
                                  start=True, stop=q0 > 0)
                    if q0 == 0:
                        m = pe.matmul(ps[:, n * w:n * w + P], mask_l, mask_r[:, 1, :], start=False, stop=True)
                m.then_inc(s_ready, 1)

            def values(j, piece, b):
                a, z = pieces(j)[piece]
                for lo in range(a - a % 512, z, 512):
                    c, q0, q1 = lo // 512, max(a, lo), min(z, lo + 512)
                    for h in range(GH):
                        m = pe.matmul(pv[c][32 * h:32 * h + 32, q0 - lo:q1 - lo], vt[b][:, j, h, :], probs[j % 2][:, h, q0 - P * j:q1 - P * j],
                                      start=(j == 0), stop=(j == 4 * c + 3))
                if z == S:
                    m.then_inc(v_done, 1)

            def turn_outputs(n):
                pe.wait_ge(o_copied, n)
                for i in range(NB):
                    m = pe.transpose(pv[i // 4][:, (i % 4) * P:(i % 4 + 1) * P], oT[:, i * P:(i + 1) * P], ident_f[:])
                m.then_inc(o_turned, 1)

            def turn_maxima(n):
                pe.wait_ge(neg2, n)
                pe.matmul(bank[SLOT["T", 0]][:, 0:64].bitcast(F16), neg_max[:], ident[:],
                          is_transpose=True, start=True, stop=True).then_inc(turned, 1)

            pe.wait_ge(ones_set, 3)
            pe.wait_ge(step_, BOTH_AT)
            pe.matmul(bank[6][:, 0:NT * E], rank_w[:, 0, :], both[:].rearrange("p t e -> p (t e)"), start=True, stop=True)
            pe.matmul(bank[7][:, 0:NT * E], rank_w[:, 1, :], both[:].rearrange("p t e -> p (t e)"), start=True, stop=True).then_inc(ranked, 1)
            pe.wait_ge(step_, ROUTED)
            pe.wait_ge(zeroed, 1)
            for c in range(2):
                m = pe.matmul(pv[c], ones[:, 0:P], ones[:], start=True, stop=c == 0)
            m.then_inc(v_done, NB - 2)
            pe.wait_ge(load[0], 64)
            pe.wait_ge(zeroed, 10)
            for k in range(NU):
                earlier = [n for n in range(k) if SLOT["M", n] == SLOT["M", k]]
                if earlier:
                    pe.wait_ge(m_taken, earlier[-1] + 1)
                maxima(k, 0)
            pe.wait_ge(m_taken, NU)
            turn_maxima(1)
            pe.wait_ge(rows_copied, 1)
            pe.wait_ge(load[1], 64)
            for k in range(LEAD):
                earlier = [n for n in range(k) if SLOT["M", n] == SLOT["M", k]]
                if earlier:
                    pe.wait_ge(m_taken, NU + earlier[-1] + 1)
                maxima(k, 1)
            pe.wait_ge(load[2], 64)

            def step(g, u, next_max, after_next, matrices):
                seq = SEQ if after_next else BEFORE_LAST_SEQ if next_max else LAST_SEQ
                before = SEQ if next_max else BEFORE_LAST_SEQ
                for at, (kind, k, x) in enumerate(seq):
                    if kind in "MST":
                        (pk, pn, px), back = previous(seq, before, at)
                        if pk == "M":
                            pe.wait_ge(m_taken, g.times(NU, NU * (px - back) + pn + 1))
                        elif pk == "S":
                            pe.wait_ge(s_taken, g.times(NU, NU * (1 - back) + pn + 1))
                        else:
                            pe.wait_ge(rows_copied, g.times(1, 2 - back))
                    if kind == "M":
                        if k == 0:
                            pe.wait_ge(load[(u + x) % 3], (g + x).thirds(64, 64))
                        maxima(k, (u + x) % 3)
                    elif kind == "T":
                        turn_maxima(g.times(1, 2))
                    elif kind == "S":
                        if k == 0:
                            pe.wait_ge(rows_in[u], g.thirds(64, 64))
                        scores(k, u)
                    elif kind == "O":
                        turn_outputs(g.times(1, 1))
                    elif k >= NB - 2:
                        pe.wait_ge(s_taken, g.times(NU, last_unit(k) + 1))
                        values(k, x, (u - 1) % 3)
                    else:
                        if k == 0 and x == 0:
                            pe.wait_ge(o_done, g.times(1, 1))
                        if x == 0:
                            pe.wait_ge(s_taken, g.times(NU, NU + last_unit(k) + 1))
                        values(k, x, u)
            walk(pe, step)
            for j in (NB - 2, NB - 1):
                pe.wait_ge(s_taken, NU * GROUPS + last_unit(j) + 1)
                values(j, 0, (GROUPS - 1) % 3)
            turn_outputs(GROUPS + 1)



class Half:

    def __init__(self, loop, at):
        self.loop, self.at = loop, at

    def __sub__(self, k):
        return Half(self.loop, self.at - k)

    def times(self, k, plus=0):
        return self.at * k + plus if self.loop is None else self.loop * (2 * k) + (self.at * k + plus)

    def halves(self, k, plus=0):
        n = self.at // 2 * k + plus
        return n if self.loop is None else self.loop * k + n


def experts(nc, psum, w_all, escale, expert_of, ident, xg_d, y_d):
    with ExitStack() as ctx:
        def sb(name, shape, dt):
            return ctx.enter_context(nc.sbuf_tensor(name, shape, dt))

        def sem(name):
            return ctx.enter_context(nc.semaphore("ex_" + name))
        B2 = SLOT_BLOCK
        xg = sb("xg", [P, 2, 2, 2 * D], F16)
        xgT = sb("xgT", [P, 2, 4, B2], F16)
        sil = sb("sil", [P, 2, 2 * B2], F32)
        hf = sb("hf", [P, 2, 2 * B2], F32)
        hh = sb("hh", [P, 2, 4, B2], F16)
        hl = sb("hl", [P, 2, 4, B2], F16)
        ysb = sb("ysb", [P, 2, 2, D], F32)
        x_in = [sem(f"x_in{n}") for n in range(2)]
        y_out = [sem(f"y_out{n}") for n in range(2)]
        x_turned, xT_done, up_done, silu_done, h_done, hi_done, lo_done, down_done, y_done, passed_ = (
            sem(n) for n in "x_turned xT_done up_done silu_done h_done hi_done lo_done down_done y_done passed".split())
        ps_x = [psum[:, n, :].bitcast(F16).rearrange("p (c t) -> p c t", c=4) for n in (6, 7)]
        ps_1 = [psum[:, n, :] for n in (0, 1)]
        ps_3 = [psum[:, n, :] for n in (2, 3)]
        ps_y = [psum[:, n, :].rearrange("p (r d) -> p r d", r=2) for n in (4, 5)]
        block = ctx.enter_context(nc.Block())
        PEELED = 5
        assert (NBLK - PEELED) % 2 == 0

        def walk(eng, step):
            for n in range(PEELED):
                step(Half(None, n), n % 2)
            with eng.Fori(0, (NBLK - PEELED) // 2) as i:
                for u in range(2):
                    step(Half(i, PEELED + u), (PEELED + u) % 2)
            for n in range(NBLK, NBLK + 2):
                step(Half(None, n), n % 2)

        def live(n):
            return n.loop is not None or 0 <= n.at < NBLK

        def after(eng, signal, n):
            if not isinstance(n, int) or n > 0:
                eng.wait_ge(signal, n)

        @block.sync
        def _(sp):
            def passed(n):
                if n.loop is not None:
                    sp.sem_inc(passed_, 1)

            def step(n, u):
                t = n - 2
                ahead, row = n.times(B2), t.times(B2)
                if n.loop is not None:
                    ahead, row = sp.snap(ahead), sp.snap(row)
                if live(n):
                    after(sp, x_turned, n.times(1, -1))
                    passed(n)
                    sp.dma_start(xg[:, u], xg_d[bass.ds(ahead, B2), :].rearrange("(r p) c -> p r c", p=P)).then_inc(x_in[u], 16)
                if live(t):
                    sp.wait_ge(y_done, t.times(1, 1))
                    passed(t)
                    sp.dma_start(y_d[bass.ds(row, B2), :].rearrange("(r p) c -> p r c", p=P), ysb[:, u]).then_inc(y_out[u], 16)
            walk(sp, step)
            sp.wait_ge(y_out[0], 16 * ((NBLK + 1) // 2))
            sp.wait_ge(y_out[1], 16 * (NBLK // 2))

        @block.scalar
        def _(act):
            def step(n, u):
                t, b = n - 1, (u - 1) % 2

                def silu(half):
                    act.wait_ge(up_done, t.times(2, half + 1))
                    after(act, h_done, t.times(2, half - 1))
                    act.activation(sil[:, half], ps_1[half], ACT.Silu, scale=escale[:, 0:1]).then_inc(silu_done, 1)

                def hi(half):
                    act.wait_ge(h_done, t.times(2, half + 1))
                    after(act, down_done, t.times(1, -1))
                    act.activation(hh[:, b, 2 * half:2 * half + 2].rearrange("p c t -> p (c t)"), hf[:, half], ACT.Copy).then_inc(hi_done, 1)
                if live(t):
                    silu(0)
                    hi(0)
                    silu(1)
                if live(n):
                    act.wait_ge(x_turned, n.times(1, 1))
                    after(act, up_done, n.times(2, -2))
                    act.activation(xgT[:, u], ps_x[u], ACT.Copy).then_inc(xT_done, 1)
                if live(t):
                    hi(1)
                t = n - 2
                if live(t):
                    act.wait_ge(down_done, t.times(1, 1))
                    after(act, y_out[u], t.halves(16))
                    act.activation(ysb[:, u], ps_y[u], ACT.Copy, scale=escale[:, 2:3]).then_inc(y_done, 1)
            walk(act, step)

        @block.vector
        def _(dve):
            def step(n, u):
                t, b = n - 1, (u - 1) % 2
                if live(t):
                    for half in range(2):
                        dve.wait_ge(silu_done, t.times(2, half + 1))
                        after(dve, lo_done, t.times(2, half - 1))
                        dve.scalar_tensor_tensor(out=hf[:, half], in0=ps_3[half], scalar=escale[:, 1:2], in1=sil[:, half], op0=ALU.mult, op1=ALU.mult).then_inc(h_done, 1)
                        dve.wait_ge(hi_done, t.times(2, half + 1))
                        dve.tensor_tensor(hl[:, b, 2 * half:2 * half + 2].rearrange("p c t -> p (c t)"), hf[:, half],
                                          hh[:, b, 2 * half:2 * half + 2].rearrange("p c t -> p (c t)"), ALU.subtract).then_inc(lo_done, 1)
            walk(dve, step)

        @block.tensor
        def _(pe):
            def step(n, u):
                t, b = n - 1, (u - 1) % 2
                if live(t):
                    e = pe.value_load(expert_of[0:1, bass.ds(t.times(1), 1)], min_val=0, max_val=E - 1)
                    pe.wait_ge(xT_done, t.times(1, 1))
                    for half in range(2):
                        after(pe, h_done, t.times(2, half - 1))
                        for w, ps in ((0, ps_1[half]), (1, ps_3[half])):
                            for c in range(2 * half, 2 * half + 2):
                                k_ = 0
                                for k in range(2):
                                    for (part, xo) in ((0, 0), (0, 2), (1, 0)):
                                        at = w * 1024 + k * 512 + c * P
                                        m = pe.matmul(ps[:, c % 2 * B2:(c % 2 + 1) * B2], w_all[:, e, part, at:at + P],
                                                      xgT[:, b, xo + k, :], start=k_ == 0, stop=k_ == 5)
                                        k_ += 1
                        m.then_inc(up_done, 1)
                if live(n):
                    pe.wait_ge(x_in[u], n.halves(16, 16))
                    after(pe, xT_done, n.times(1, -1))
                    for c in range(4):
                        for r in range(2):
                            m = pe.matmul(ps_x[u][:, c, r * P:(r + 1) * P], xg[:, u, r, c * P:(c + 1) * P], ident[:], is_transpose=True, start=True, stop=True)
                    m.then_inc(x_turned, 1)
                t = n - 2
                if live(t):
                    e = pe.value_load(expert_of[0:1, bass.ds(t.times(1), 1)], min_val=0, max_val=E - 1)
                    pe.wait_ge(lo_done, t.times(2, 2))
                    after(pe, y_done, t.times(1, -1))
                    for r in range(2):
                        k_ = 0
                        for c in range(4):
                            for (hx, part) in ((hh, 0), (hl, 0), (hh, 1)):
                                m = pe.matmul(ps_y[u][:, r], hx[:, u, c, r * P:(r + 1) * P], w_all[:, e, part, 2048 + c * D:2048 + (c + 1) * D], start=k_ == 0, stop=k_ == 11)
                                k_ += 1
                    m.then_inc(down_done, 1)
            walk(pe, step)


def ending(nc, psum, x, o_d, y_d, woutt, out, ident_f, gates, slot_of):
    with ExitStack() as ctx:
        def sb(name, shape, dt):
            return ctx.enter_context(nc.sbuf_tensor(name, shape, dt))

        def sem(name):
            return ctx.enter_context(nc.semaphore("en_" + name))
        wo = sb("wo", [P, 2, D], F32)
        xs = sb("xs", [P, 4, D], F32)
        os_ = sb("os", [P, 4, D], F32)
        oT = sb("oTe", [P, 2, 2, P], F32)
        y = sb("y", [P, 8, 2, D], F32)
        f1 = sb("f1", [P, 2, D], F32)
        f2 = sb("f2", [P, 2, D], F32)
        sg = sb("sg", [P, 2, D], F32)
        r1 = sb("r1", [P, 2, D], F32)
        r2 = sb("r2", [P, 4, D], F32)
        x_in = [sem(f"x_in{n}") for n in range(4)]
        y_in = [sem(f"y_in{n}") for n in range(8)]
        outs = [sem(f"out{n}") for n in range(4)]
        w_in, o_turned, oT_done, s_done, f1_done, f2_done, g_done, r1_done, r2_done, passed_ = (
            sem(n) for n in "w_in o_turned oT_done s_done f1_done f2_done g_done r1_done r2_done passed".split())
        ps_t = [psum[:, n, 0:D] for n in (0, 1)]
        ps_s = [psum[:, n, 0:D] for n in (2, 3)]
        block = ctx.enter_context(nc.Block())
        PRODUCT, SUM, SILU, LAST, STORE = 1, 0, 1, 2, 3

        def walk(eng, step):
            for n in range(8):
                step(Count(None, n), n)
            with eng.Fori(0, (NT - 8) // 8) as i:
                for u in range(8):
                    step(Eighth(i, 8 + u), u)
            for n in range(NT, NT + STORE):
                step(Count(None, n), n % 8)

        def live(n):
            return n.loop is not None or 0 <= n.at < NT

        def after(eng, signal, n):
            if not isinstance(n, int) or n > 0:
                eng.wait_ge(signal, n)

        @block.sync
        def _(sp):
            def passed(n):
                if n.loop is not None:
                    sp.sem_inc(passed_, 1)
            sp.dma_start(wo[:], woutt.rearrange("(c p) n -> p c n", p=P)).then_inc(w_in, 16)

            def step(n, u):
                t = n - STORE
                ahead, row = n.times(P), t.times(P)
                if n.loop is not None:
                    ahead, row = sp.snap(ahead), sp.snap(row)
                if live(n):
                    after(sp, r2_done, n.times(1, -3))
                    passed(n)
                    sp.dma_start(xs[:, u % 4], x[bass.ds(ahead, P), :]).then_inc(x_in[u % 4], 16)
                    sp.dma_start(os_[:, u % 4], o_d[bass.ds(ahead, P), :]).then_inc(x_in[u % 4], 16)
                if live(t):
                    b = (u - STORE) % 4
                    sp.wait_ge(r2_done, t.times(1, 1))
                    passed(t)
                    sp.dma_start(out[bass.ds(row, P), :], r2[:, b]).then_inc(outs[b], 16)
            walk(sp, step)
            for n in range(4):
                sp.wait_ge(outs[n], 4 * NT)

        @block.gpsimd
        def _(pool):
            for t in range(NT):
                if t >= 8:
                    pool.wait_ge(f2_done, t - 7)
                for k in range(2):
                    pool.indirect_dma_start(out=y[:, t % 8, k, :], out_offset=None, in_=y_d,
                                            in_offset=bass.IndirectOffsetOnAxis(ap=slot_of[:, k, t:t + 1], axis=0)).then_inc(y_in[t % 8], 16)

        @block.scalar
        def _(act):
            def step(n, u):
                if live(n):
                    act.wait_ge(o_turned, n.times(1, 1))
                    after(act, s_done, n.times(1, -1))
                    act.activation(oT[:, u % 2].rearrange("p c t -> p (c t)"), ps_t[u % 2], ACT.Copy).then_inc(oT_done, 1)
                t, b = n - SILU, (u - SILU) % 2
                if live(t):
                    act.wait_ge(f2_done, t.times(1, 1))
                    after(act, r1_done, t.times(1, -1))
                    act.activation(sg[:, b], f2[:, b], ACT.Silu).then_inc(g_done, 1)
            walk(act, step)

        @block.vector
        def _(dve):
            def step(n, u):
                t, b = n - LAST, (u - LAST) % 4
                if live(n):
                    dve.wait_ge(y_in[u], n.eighths(32, 32))
                    dve.tensor_scalar(f1[:, u % 2], y[:, u, 0], gates[:, 0, bass.ds(n.times(1), 1)], None, ALU.mult).then_inc(f1_done, 1)
                if live(t):
                    dve.wait_ge(s_done, t.times(1, 1))
                    dve.wait_ge(g_done, t.times(1, 1))
                    dve.tensor_tensor(r1[:, b % 2], ps_s[b % 2], sg[:, b % 2], ALU.mult).then_inc(r1_done, 1)
                if live(n):
                    dve.wait_ge(f1_done, n.times(1, 1))
                    after(dve, g_done, n.times(1, -1))
                    dve.scalar_tensor_tensor(out=f2[:, u % 2], in0=y[:, u, 1], scalar=gates[:, 1, bass.ds(n.times(1), 1)], in1=f1[:, u % 2], op0=ALU.mult, op1=ALU.add).then_inc(f2_done, 1)
                if live(t):
                    dve.wait_ge(r1_done, t.times(1, 1))
                    after(dve, outs[b], t.quarters(16))
                    dve.wait_ge(x_in[b], t.quarters(32, 32))
                    dve.tensor_tensor(r2[:, b], r1[:, b % 2], xs[:, b], ALU.add).then_inc(r2_done, 1)
            walk(dve, step)

        @block.tensor
        def _(pe):
            pe.wait_ge(w_in, 16)

            def step(n, u):
                if live(n):
                    pe.wait_ge(x_in[u % 4], n.quarters(32, 32))
                    after(pe, oT_done, n.times(1, -1))
                    for c in range(2):
                        m = pe.transpose(ps_t[u % 2][:, c * P:(c + 1) * P], os_[:, u % 4, c * P:(c + 1) * P], ident_f[:])
                    m.then_inc(o_turned, 1)
                t, b = n - PRODUCT, (u - PRODUCT) % 2
                if live(t):
                    pe.wait_ge(oT_done, t.times(1, 1))
                    after(pe, r1_done, t.times(1, -1))
                    for c in range(2):
                        m = pe.matmul(ps_s[b], oT[:, b, c, :], wo[:, c, :], start=c == 0, stop=c == 1)
                    m.then_inc(s_done, 1)
            walk(pe, step)



def moe_attention_kernel(nc, x, wqkvg, w1t, w3t, w2t, woutt, rope_cos, rope_sin, ident16, ident32, mask_values, ranks_f, small, out):
    def scratch(name, shape, dt):
        return nc.dram_tensor(name, shape, dt, kind="Internal").ap()
    qT_d, kT_d = scratch("qT_d", (H // 2, P, T), F16), scratch("kT_d", (H // 2, P, T), F16)
    v_d, o_d = scratch("v_d", (T, 32 * H), F32), scratch("o_d", (T, D), F32)
    xg_d, y_d = scratch("xg_d", (CLEARED * P * NT // 4, 2 * D), F16), scratch("y_d", (SLOTS, D), F32)
    assert SLOTS <= CLEARED * P * NT // 4
    with ExitStack() as ctx:
        def sb(name, shape, dt):
            return ctx.enter_context(nc.sbuf_tensor(name, shape, dt))
        psum = ctx.enter_context(nc.psum_tensor("psum", [P, 8, 512], F32))
        ident, ident_f, masks = sb("ident", [P, P], F16), sb("ident_f", [P, P], F32), sb("masks", [P, 3, P], BF16)
        logits, pow2 = sb("logits", [P, NT, E], F32), sb("pow2", [P, 2], F32)
        gates, slot_of = sb("gates", [P, 2, NT], F32), sb("slot_of", [P, 2, NT], I32)
        expert_of, escale = sb("expert_of", [P, NBLK], I32), sb("escale", [P, 4], F32)
        rank_f, small_sb = sb("rank_f", [P, 2, P], F32), sb("small_sb", [P, E + NBLK], F32)
        w_all = sb("w_all", [P, E, 2, WCOLS], F16)
        flat = w_all[:].rearrange("p e h w -> p (e h w)")
        xall = flat[:, 0:2 * NT * D].bitcast(F32).rearrange("p (t d) -> p t d", t=NT)
        xhl = flat[:, E * 2 * WCOLS - NT * 2 * D:].rearrange("p (t d) -> p t d", t=NT)
        bank = [psum[:, n, :] for n in range(8)]
        experts_w = (w1t, w3t, w2t)
        project(nc, bank, x, wqkvg, rope_cos, rope_sin, ident16, ident32, mask_values, qT_d, kT_d, v_d, ident, ident_f, masks,
                xall, xhl, logits, pow2, xg_d, ranks_f, small, rank_f, small_sb)
        attention(nc, psum, qT_d, kT_d, v_d, o_d, ident, ident_f, masks, pow2, w_all, xg_d, experts_w, escale, xhl, logits,
                  rank_f, small_sb, gates, slot_of, expert_of)
        experts(nc, psum, w_all, escale, expert_of, ident, xg_d, y_d)
        ending(nc, psum, x, o_d, y_d, woutt, out, ident_f, gates, slot_of)


def constants():
    rate = 1.0 / 10000.0 ** (np.arange(0, HD, 2, dtype=np.float32) / HD)
    angle = np.outer(np.arange(S, dtype=np.float32), rate)
    angle = np.concatenate([angle, angle], axis=1)
    sign = np.tile([-1.0, 1.0], HD // 2)
    r = np.arange(P)
    masks = np.zeros((P, 3, P), np.float32)
    masks[:, 0] = np.eye(P) * 2.0 ** 60
    masks[:, 1] = np.where(r[None] > r[:, None], -2.0 ** 60, 0)
    masks[:, 2] = np.where(r[None] < r[:, None], -2.0 ** 60, 0)
    ranks = np.ones((P, 2, P), np.float32)
    ranks[:, 0] = r[:, None] < r[None]
    return {
        "rope_cos": np.tile((np.cos(angle) * 2.0 ** -22).astype(np.float32), (B, 1)),
        "rope_sin": np.tile((np.sin(angle) * sign * 2.0 ** -22).astype(np.float32), (B, 1)),
        "ident16": np.eye(P, dtype=np.float16), "ident32": np.eye(P, dtype=np.float32),
        "mask_values": masks, "ranks_f": ranks,
        "small": np.tile(np.concatenate([E - np.arange(E), np.arange(NBLK)]).astype(np.float32), (P, 1)),
    }


def kernel(**inputs):
    import concourse.bacc as bacc
    from concourse.bass_utils import run_bass_kernel_spmd

    f = {k: np.asarray(v) for k, v in inputs.items()}
    arrays = {
        "x": np.ascontiguousarray(f["L0_attn_x"].reshape(T, D)),
        "wqkvg": np.ascontiguousarray(np.concatenate([f["L0_attn_Wqkv"].T, f["L0_ffn_gate_w"].T], axis=1)),
        "w1t": np.ascontiguousarray(f["L0_ffn_w1"].transpose(0, 2, 1)),
        "w3t": np.ascontiguousarray(f["L0_ffn_w3"].transpose(0, 2, 1)),
        "w2t": np.ascontiguousarray(f["L0_ffn_w2"].transpose(0, 2, 1)),
        "woutt": np.ascontiguousarray(f["L0_attn_Wout"].T),
        **constants(),
    }
    nc = bacc.Bacc("TRN2", target_bir_lowering=False, num_devices=1)
    args = {k: nc.dram_tensor("in_" + k, a.shape, mybir.dt.from_np(a.dtype), kind="ExternalInput").ap() for k, a in arrays.items()}
    out = nc.dram_tensor("out", (T, D), F32, kind="ExternalOutput").ap()
    moe_attention_kernel(nc, out=out, **args)
    r = run_bass_kernel_spmd(nc, [{"in_" + k: a for k, a in arrays.items()}], core_ids=[0])
    return r.results[0]["out"].reshape(B, S, D)
```

```python
import concourse.bass as bass
from concourse import mybir
from contextlib import ExitStack
import numpy as np

F32 = mybir.dt.float32
F16 = mybir.dt.float16
BF16 = mybir.dt.bfloat16
I32 = mybir.dt.int32
U32 = mybir.dt.uint32
ALU = mybir.AluOpType
ACT = mybir.ActivationFunctionType
AX = mybir.AxisListType.X
ABSMAX = bass.bass_isa.ReduceOp.absmax

P = 128
B, S, D = 4, 1024, 256
T = B * S
NT = T // P
H = 16
HD = D // H
E = 8
NI = 512
QG = 3 * D + E
CLEARED = 10
XCOLS = 2 * D + 2


class Count:
    STRIDE = 4

    def __init__(self, loop, at):
        self.loop, self.at = loop, at

    def __sub__(self, k):
        return type(self)(self.loop, self.at - k)

    def times(self, k, plus=0):
        return self.share(1, k, plus)

    def share(self, n, k, plus=0):
        rest = self.at // n * k + plus
        return rest if self.loop is None else self.loop * (self.STRIDE // n * k) + rest

    def quarters(self, k, plus=0):
        return self.share(4, k, plus)

    def eighths(self, k, plus=0):
        return self.share(8, k, plus)


class Eighth(Count):
    STRIDE = 8


def project(nc, bank, x, wqg, rope_cos, rope_sin, ident_h, ident32_h, masks_h, qT_d, kT_d, v_d, ident, ident_f, masks, xall, xhl, logits, pow2, xg_d, ranks_h, small_h, rank_f, small, token_ids, xhl_id):
    with ExitStack() as ctx:
        def sb(name, shape, dt):
            return ctx.enter_context(nc.sbuf_tensor(name, shape, dt))

        def sem(name):
            return ctx.enter_context(nc.semaphore(name))

        wqg_f = sb("wqg_f", [P, 2, QG], F32)
        wqg_h = sb("wqg_h", [P, 2, QG], F16)
        wqg_l = sb("wqg_l", [P, 2, QG], F16)
        cos_sb = sb("cos_sb", [P, NT, HD], F32)
        sin_sb = sb("sin_sb", [P, NT, HD], F32)
        masks_f = sb("masks_f", [P, 3, P], F32)
        amax = sb("amax", [P, 2], F32)
        amax_all = sb("amax_all", [P, 2], F32)
        rscale = sb("rscale", [P, 2], F32)
        stats = sb("stats", [P, NT, 6], F32)
        mv = sb("mv", [P, NT, 2], F32)
        rstd = sb("rstd", [P, 4, NT], F32)
        zeros = sb("zeros", [P, 1, XCOLS], F16)
        ids = sb("ids", [P, NT], I32)
        eps = sb("eps", [P, 1], F32)
        xn = sb("xn", [P, 2, D], F32)
        xT = sb("xT", [P, 2, 4, P], F16)
        ra = sb("ra", [P, 2, 512], F32)
        rb = sb("rb", [P, 2, 512], F32)
        qk = sb("qk", [P, 4, 512], F32)
        qaug = sb("qaug", [P, 2, H, 4, HD], F16)
        kaug = sb("kaug", [P, 2, H, 4, HD], F16)
        vaug = sb("vaug", [P, 4, H, 32], F32)
        qst = sb("qst", [P, 2, 8, 2 * P], F16)
        kst = sb("kst", [P, 2, 8, 2 * P], F16)

        names = """const_in w_in x_in0 x_in1 x_in2 x_in3 amax_done amax_sum weight_done set_done v_zero bn_stats bn_aggr std rstd
                   xn_done hi_done lo_done xtr_done xT_done qkv_done rope_done qk_done v_done lg_done qk_hi qk_lo aug_done q_evac k_evac
                   q_out0 q_out1 k_out0 k_out1 v_out0 v_out1 v_out2 v_out3 sp_passed zero_set zero_out late_in""".split()
        s = {n: sem(n) for n in names}

        ps_x = [bank[0], bank[1]]
        ps_qk = [bank[2], bank[3]]
        ps_vg = [bank[4], bank[5]]
        ps_tq, ps_tk = bank[6], bank[7]
        TURN, PRODUCT, ROPE, HALVES, REST, STORE = 1, 2, 3, 4, 5, 6
        PEELED = 8
        FIRST = 8

        def pipeline(eng, step):
            for n in range(PEELED):
                step(Count(None, n), n % 4)
            with eng.Fori(0, (NT - PEELED) // 4) as i:
                for u in range(4):
                    step(Count(i, PEELED + u), u)
            for n in range(NT, NT + STORE):
                step(Count(None, n), n % 4)

        def live(n):
            return n.loop is not None or 0 <= n.at < NT

        def after(eng, signal, n):
            if not isinstance(n, int) or n > 0:
                eng.wait_ge(signal, n)

        block = ctx.enter_context(nc.Block())

        @block.sync
        def _(sp):
            for n in ("q_out0", "q_out1", "k_out0", "k_out1"):
                sp.sem_inc(s[n], 16)
            sp.dma_start(wqg_f[:], wqg.rearrange("(c p) n -> p c n", p=P)).then_inc(s["w_in"], 16)
            for c in range(4):
                r = NT // 4
                sp.dma_start(xall[:, c * r:(c + 1) * r, :], x[c * r * P:(c + 1) * r * P, :].rearrange("(t p) d -> p t d", p=P)).then_inc(s["x_in%d" % c], 16)
            sp.dma_start(ident[:], ident_h).then_inc(s["const_in"], 16)
            sp.dma_start(ident_f[:], ident32_h).then_inc(s["const_in"], 16)
            sp.dma_start(masks_f[:], masks_h).then_inc(s["const_in"], 16)
            sp.dma_start(cos_sb[:], rope_cos.rearrange("(t p) d -> p t d", p=P)).then_inc(s["const_in"], 16)
            sp.dma_start(sin_sb[:], rope_sin.rearrange("(t p) d -> p t d", p=P)).then_inc(s["const_in"], 16)

            sp.dma_start(rank_f[:], ranks_h).then_inc(s["late_in"], 16)
            sp.dma_start(small[:], small_h).then_inc(s["late_in"], 16)
            sp.dma_start(ids[:], token_ids).then_inc(s["late_in"], 16)
            sp.wait_ge(s["zero_set"], 1)

            def passed(n):
                if n.loop is not None:
                    sp.sem_inc(s["sp_passed"], 1)

            def step(n, u):
                tv, tq = n - ROPE, n - STORE
                row, pair, clear = tv.times(P), (tq - 1).times(P), n.quarters(CLEARED * P)
                if n.loop is not None:
                    row, pair, clear = sp.snap(row), sp.snap(pair), sp.snap(clear)
                if live(n) and u == 3:
                    sp.dma_start(xg_d[bass.ds(clear, CLEARED * P), :].rearrange("(p r) c -> p r c", r=CLEARED),
                                 zeros[:].broadcast_to([P, CLEARED, XCOLS])).then_inc(s["zero_out"], 16)
                if live(tv):
                    v = (u - ROPE) % 4
                    sp.wait_ge(s["v_done"], tv.times(1, 1))
                    passed(tv)
                    sp.dma_start(v_d[bass.ds(row, P), :], vaug[:, v].rearrange("p h d -> p (h d)")).then_inc(s["v_out%d" % v], 16)
                v = (u - STORE) % 4
                if live(tq) and v % 2:
                    sp.wait_ge(s["q_evac"], tq.times(1, 1))
                    passed(tq)
                    sp.dma_start(qT_d[:, :, bass.ds(pair, 2 * P)].rearrange("h p t -> p h t"), qst[:, v // 2]).then_inc(s["q_out%d" % (v // 2)], 16)
                    sp.wait_ge(s["k_evac"], tq.times(1, 1))
                    passed(tq)
                    sp.dma_start(kT_d[:, :, bass.ds(pair, 2 * P)].rearrange("h p t -> p h t"), kst[:, v // 2]).then_inc(s["k_out%d" % (v // 2)], 16)
            pipeline(sp, step)
            sp.wait_ge(s["late_in"], 48)
            sp.wait_ge(s["zero_out"], 16 * (NT // 4))
            for n in range(4):
                sp.wait_ge(s["v_out%d" % n], 4 * NT)
            for n in range(2):
                sp.wait_ge(s["q_out%d" % n], 4 * NT + 16)
                sp.wait_ge(s["k_out%d" % n], 4 * NT + 16)

        @block.gpsimd
        def _(pool):
            pool.memset(zeros[:], 0.0).then_inc(s["zero_set"], 1)
            pool.memset(eps[:], 1e-5).then_inc(s["set_done"], 1)
            pool.memset(qaug[:, :, :, 3, :], 0.0).then_inc(s["set_done"], 1)
            pool.memset(kaug[:, :, :, 3, 2:HD], 0.0).then_inc(s["set_done"], 1)
            pool.memset(kaug[:, :, :, 3, 0:2], 32768.0).then_inc(s["set_done"], 1)
            pool.memset(vaug[:, :, :, HD:32], 0.0).then_inc(s["v_zero"], 1)
            pool.wait_ge(s["v_zero"], 1)
            pool.memset(vaug[:, :, :, HD], 1.0).then_inc(s["set_done"], 1)
            pool.wait_ge(s["amax_done"], 2)
            pool.partition_all_reduce(amax_all[:], amax[:], P, ABSMAX).then_inc(s["amax_sum"], 1)
            pool.wait_ge(s["const_in"], 80)
            pool.tensor_copy(masks[:], masks_f[:])

            def step(n, u):
                t, b, v = n - ROPE, (u - ROPE) % 2, (u - ROPE) % 4
                if live(t):
                    pool.wait_ge(s["rope_done"], t.times(2, 2))
                    after(pool, s["qk_lo"], t.times(2, -6))
                    pool.tensor_tensor(qk[:, v], ra[:, b], rb[:, b], ALU.add).then_inc(s["qk_done"], 1)
                if live(n):
                    pool.wait_ge(s["hi_done"], n.times(1, 1))
                    pool.tensor_tensor(xhl[:, n.times(1), D:2 * D], xn[:, u % 2], xhl[:, n.times(1), 0:D], ALU.subtract).then_inc(s["lo_done"], 1)
            pipeline(pool, step)
            pool.wait_ge(s["late_in"], 48)
            pool.tensor_copy(xhl_id, ids[:])

        @block.scalar
        def _(act):
            act.wait_ge(s["set_done"], 5)

            def roots(a, z):
                act.wait_ge(s["bn_aggr"], z)
                act.activation(rstd[:, 0, a:z], mv[:, a:z, 1], ACT.Sqrt, bias=eps[:, 0:1]).then_inc(s["std"], 1)
            roots(0, FIRST)

            def step(n, u):
                if n.loop is None and n.at == PEELED - 1:
                    roots(FIRST, NT)
                t, b = n - PRODUCT, (u - PRODUCT) % 2
                if live(t):
                    act.wait_ge(s["xtr_done"], t.times(1, 1))
                    after(act, s["qkv_done"], t.times(1, -1))
                    act.activation(xT[:, b].rearrange("p c t -> p (c t)"), ps_x[b][:, 0:256].bitcast(F16), ACT.Copy).then_inc(s["xT_done"], 1)
                t, b, v = n - ROPE, (u - ROPE) % 2, (u - ROPE) % 4
                if live(t):
                    act.wait_ge(s["qkv_done"], t.times(1, 1))
                    after(act, s["v_out%d" % v], t.quarters(16))
                    act.activation(vaug[:, v, :, 0:HD], ps_vg[b][:, 0:D].rearrange("p (h d) -> p h d", d=HD), ACT.Copy).then_inc(s["v_done"], 1)
                    act.activation(logits[:, t.times(1), :], ps_vg[b][:, D:D + E], ACT.Copy).then_inc(s["lg_done"], 1)
                t, c, h = n - STORE, ((u - STORE) % 4) // 2, ((u - STORE) % 2) * P
                if live(t):
                    act.wait_ge(s["aug_done"], t.times(1, 1))
                    act.wait_ge(s["q_out%d" % c], t.quarters(16, 16))
                    act.activation(qst[:, c, :, h:h + P], ps_tq[:].bitcast(F16).rearrange("p (h t) -> p h t", h=8), ACT.Copy).then_inc(s["q_evac"], 1)
                t, b, v = n - HALVES, (u - HALVES) % 2, (u - HALVES) % 4
                if live(t):
                    act.wait_ge(s["qk_done"], t.times(1, 1))
                    after(act, s["aug_done"], t.times(1, -1))
                    q3 = qk[:, v, 0:D].rearrange("p (h o d) -> p h o d", o=1, d=HD).broadcast_to([P, H, 2, HD])
                    k3 = qk[:, v, D:2 * D].rearrange("p (h o d) -> p h o d", o=1, d=HD).broadcast_to([P, H, 2, HD])
                    act.activation(qaug[:, b, :, 0:2, :], q3, ACT.Copy).then_inc(s["qk_hi"], 1)
                    act.activation(kaug[:, b, :, 0:3:2, :], k3, ACT.Copy).then_inc(s["qk_hi"], 1)
                if live(n):
                    act.wait_ge(s["xn_done"], n.times(1, 1))
                    act.activation(xhl[:, n.times(1), 0:D], xn[:, u % 2], ACT.Copy).then_inc(s["hi_done"], 1)
            pipeline(act, step)

        @block.vector
        def _(dve):
            dve.wait_ge(s["w_in"], 16)
            dve.tensor_reduce(amax[:, 0:1], wqg_f[:, :, 0:3 * D], mybir.AxisListType.XY, ALU.max, apply_absolute_value=True).then_inc(s["amax_done"], 1)
            dve.tensor_reduce(amax[:, 1:2], wqg_f[:, :, 3 * D:QG], mybir.AxisListType.XY, ALU.max, apply_absolute_value=True).then_inc(s["amax_done"], 1)

            def statistics(a, z):
                for t in range(a, z):
                    dve.wait_ge(s["x_in%d" % (t * 4 // NT)], 16)
                    dve.bn_stats(stats[:, t], xall[:, t]).then_inc(s["bn_stats"], 1)
            statistics(0, FIRST)
            dve.wait_ge(s["amax_sum"], 1)
            dve.tensor_scalar(rscale[:], amax_all[:], 2.0 ** -100, None, ALU.max).then_inc(s["weight_done"], 1)
            dve.wait_ge(s["weight_done"], 1)
            dve.tensor_scalar(pow2[:].bitcast(U32), rscale[:].bitcast(U32), 0x7F800000, None, ALU.bitwise_and).then_inc(s["weight_done"], 1)
            dve.wait_ge(s["weight_done"], 2)
            dve.reciprocal(rscale[:], pow2[:]).then_inc(s["weight_done"], 1)
            dve.wait_ge(s["weight_done"], 3)
            dve.tensor_scalar(rscale[:], rscale[:], 2.0 ** 14, None, ALU.mult).then_inc(s["weight_done"], 1)
            dve.wait_ge(s["weight_done"], 4)
            for n, (a, z) in enumerate(((0, 3 * D), (3 * D, QG))):
                dve.tensor_scalar(wqg_h[:, :, a:z], wqg_f[:, :, a:z], rscale[:, n:n + 1], None, ALU.mult).then_inc(s["weight_done"], 1)
            dve.wait_ge(s["weight_done"], 6)
            for n, (a, z) in enumerate(((0, 3 * D), (3 * D, QG))):
                dve.scalar_tensor_tensor(out=wqg_l[:, :, a:z], in0=wqg_f[:, :, a:z], scalar=rscale[:, n:n + 1], in1=wqg_h[:, :, a:z],
                                         op0=ALU.mult, op1=ALU.subtract).then_inc(s["weight_done"], 1)

            def aggregate(a, z):
                for t in range(a, z):
                    dve.wait_ge(s["bn_stats"], t + 1)
                    dve.bn_aggr(mv[:, t], stats[:, t]).then_inc(s["bn_aggr"], 1)

            def invert(a, z, turn):
                dve.wait_ge(s["std"], turn + 1)
                dve.reciprocal(rstd[:, 1, a:z], rstd[:, 0, a:z]).then_inc(s["rstd"], 1)
                dve.wait_ge(s["rstd"], 5 * turn + 1)
                dve.tensor_tensor(rstd[:, 2, a:z], rstd[:, 1, a:z], rstd[:, 1, a:z], ALU.mult).then_inc(s["rstd"], 1)
                dve.wait_ge(s["rstd"], 5 * turn + 2)
                dve.scalar_tensor_tensor(out=rstd[:, 3, a:z], in0=mv[:, a:z, 1], scalar=1e-5, in1=rstd[:, 2, a:z], op0=ALU.add, op1=ALU.mult).then_inc(s["rstd"], 1)
                dve.wait_ge(s["rstd"], 5 * turn + 3)
                dve.tensor_scalar(rstd[:, 2, a:z], rstd[:, 3, a:z], -0.5 * 2048, 1.5 * 2048, ALU.mult, ALU.add).then_inc(s["rstd"], 1)
                dve.wait_ge(s["rstd"], 5 * turn + 4)
                dve.tensor_tensor(rstd[:, 0, a:z], rstd[:, 1, a:z], rstd[:, 2, a:z], ALU.mult).then_inc(s["rstd"], 1)
                dve.wait_ge(s["rstd"], 5 * turn + 5)
            aggregate(0, FIRST)
            invert(0, FIRST, 0)

            def step(n, u):
                if live(n):
                    after(dve, s["lo_done"], n.times(1, -1))
                    dve.tensor_scalar(xn[:, u % 2], xall[:, n.times(1)], mv[:, n.times(1), 0:1], rstd[:, 0, bass.ds(n.times(1), 1)], ALU.subtract, ALU.mult).then_inc(s["xn_done"], 1)
                t, b, v = n - REST, (u - REST) % 2, (u - REST) % 4
                if live(t):
                    dve.wait_ge(s["qk_hi"], t.times(2, 2))
                    for (aug, part, o) in ((qaug, 2, 0), (kaug, 1, D)):
                        dve.tensor_tensor(aug[:, b, :, part, :], qk[:, v, o:o + D].rearrange("p (h d) -> p h d", d=HD), aug[:, b, :, 0, :],
                                          ALU.subtract).then_inc(s["qk_lo"], 1)
                t, b = n - ROPE, (u - ROPE) % 2
                if live(t):
                    dve.wait_ge(s["qkv_done"], t.times(1, 1))
                    after(dve, s["qk_done"], t.times(1, -1))
                    src = ps_qk[b][:].rearrange("p (h d) -> p h d", d=HD)
                    cs = cos_sb[:, t.times(1), :].rearrange("p (o d) -> p o d", o=1).broadcast_to([P, 2 * H, HD])
                    dve.tensor_tensor(ra[:, b].rearrange("p (h d) -> p h d", d=HD), src, cs, ALU.mult).then_inc(s["rope_done"], 1)
                    sn = sin_sb[:, t.times(1), :].rearrange("p (o d e) -> p o d e", o=1, e=2).broadcast_to([P, 2 * H, HD // 2, 2])
                    rot = ps_qk[b][:].rearrange("p (h d e) -> p h d e", d=HD // 2, e=2)[:, :, :, ::-1]
                    dve.tensor_tensor(rb[:, b].rearrange("p (h d e) -> p h d e", d=HD // 2, e=2), rot, sn, ALU.mult).then_inc(s["rope_done"], 1)
                t, c, h = n - STORE, ((u - STORE) % 4) // 2, ((u - STORE) % 2) * P
                if live(t):
                    dve.wait_ge(s["aug_done"], t.times(1, 1))
                    dve.wait_ge(s["k_out%d" % c], t.quarters(16, 16))
                    dve.tensor_copy(kst[:, c, :, h:h + P], ps_tk[:].bitcast(F16).rearrange("p (h t) -> p h t", h=8)).then_inc(s["k_evac"], 1)
                if n.loop is None and n.at < PEELED:
                    if n.at < PEELED - 2:
                        statistics(FIRST + 4 * n.at, FIRST + 4 * n.at + 4)
                    elif n.at == PEELED - 2:
                        aggregate(FIRST, NT)
                    else:
                        invert(FIRST, NT, 1)
            pipeline(dve, step)

        @block.tensor
        def _(pe):
            pe.wait_ge(s["weight_done"], 8)
            pe.wait_ge(s["const_in"], 80)

            def step(n, u):
                t, b = n - TURN, (u - TURN) % 2
                if live(t):
                    pe.wait_ge(s["lo_done"], t.times(1, 1))
                    after(pe, s["xT_done"], t.times(1, -1))
                    for c in range(4):
                        m = pe.matmul(ps_x[b][:, 0:256].bitcast(F16)[:, c * P:(c + 1) * P], xhl[:, t.times(1), c * P:(c + 1) * P], ident[:],
                                      is_transpose=True, start=True, stop=True)
                    m.then_inc(s["xtr_done"], 1)
                t, b = n - PRODUCT, (u - PRODUCT) % 2
                if live(t):
                    pe.wait_ge(s["xT_done"], t.times(1, 1))
                    after(pe, s["rope_done"], t.times(2, -2))
                    after(pe, s["lg_done"], t.times(1, -1))
                    terms = [(0, wqg_h), (0, wqg_l), (2, wqg_h)]
                    for k in range(2):
                        for m_, (xo, w) in enumerate(terms):
                            first, last = k == 0 and m_ == 0, k == 1 and m_ == 2
                            pe.matmul(ps_qk[b][:], xT[:, b, xo + k], w[:, k, 0:512], start=first, stop=last)
                            m = pe.matmul(ps_vg[b][:, 0:QG - 512], xT[:, b, xo + k], w[:, k, 512:QG], start=first, stop=last)
                    m.then_inc(s["qkv_done"], 1)
                t, b = n - REST, (u - REST) % 2
                if live(t):
                    pe.wait_ge(s["qk_lo"], t.times(2, 2))
                    after(pe, s["q_evac"], t.times(1))
                    after(pe, s["k_evac"], t.times(1))
                    for aug, ps in ((qaug, ps_tq), (kaug, ps_tk)):
                        for c in range(8):
                            m = pe.matmul(ps[:].bitcast(F16)[:, c * P:(c + 1) * P], aug[:, b, 2 * c:2 * c + 2].rearrange("p h e d -> p (h e d)"), ident[:],
                                          is_transpose=True, start=True, stop=True)
                    m.then_inc(s["aug_done"], 1)
            pipeline(pe, step)


GROUPS = 16
GH = 4
NB = S // P


class Group:

    def __init__(self, loop, at):
        self.loop, self.at = loop, at

    def __add__(self, k):
        return Group(self.loop, self.at + k)

    def times(self, k, plus=0):
        return self.at * k + plus if self.loop is None else self.loop * (3 * k) + (self.at * k + plus)

    def thirds(self, k, plus=0):
        n = self.at // 3 * k + plus
        return n if self.loop is None else self.loop * k + n


class Matrix:

    def __init__(self, loop, each, at):
        self.loop, self.each, self.at = loop, each, at
        self.kind, self.splits = at % 3, at >= 3 * E

    def __add__(self, k):
        return Matrix(self.loop, self.each, self.at + k)

    def times(self, k, plus=0):
        return self.at * k + plus if self.loop is None else self.loop * (self.each * k) + (self.at * k + plus)

    def turns(self, k, plus=0):
        n = self.at // 3 * k + plus
        return n if self.loop is None else self.loop * (self.each // 3 * k) + n

    def expert(self, eng):
        n = self.at // 3 % E
        return n if self.loop is None else eng.snap((self.loop * (self.each // 3) + self.at // 3) % E)


SLOTS_OF = {4: (6, 16, 26, 36), 2: (10, 28), 3: (8, 20, 32)}


def width_units():
    units = []
    for j in range(NB):
        w = S - P * j
        if w > 512:
            units += [(j, [h], c, w // 2) for h in range(GH) for c in (0, w // 2)]
        else:
            per = max(1, 512 // w) if w != 384 else 1
            units += [(j, list(range(h, h + per)), 0, w) for h in range(0, GH, per)]
    return units


UNITS = width_units()
NU = len(UNITS)
LEAD = 10
RING = 6


def pieces(j):
    cuts = [c for c in (256, 512, 768) if c - P * j > P and (j > 0 or c == 512)] + [S]
    return list(zip([P * j] + cuts[:-1], cuts))


def order(next_max, after_next):
    then = {1: (NB - 2, 0), 3: (NB - 1, 0), 12: (0, 0), 14: (0, 1), 17: (1, 0), 19: (1, 1), 21: (1, 2), 25: (2, 0), 27: (2, 1), 29: (2, 2),
            33: (3, 0), 34: (3, 1), 37: (4, 0), 38: (4, 1), 41: (5, 0)}
    assert sorted(then.values()) == [(j, p) for j in range(NB) for p in range(len(pieces(j)))]
    seq = []
    for k in range(NU):
        seq.append(("S", k, 0))
        if k == 35:
            seq.append(("T", 0, 1))
        if k == 8:
            seq.append(("O", 0, 0))
        seq += [("V", *then[k])] if k in then else []
        seq.append(("M", k + LEAD, 1) if k + LEAD < NU else ("M", k + LEAD - NU, 2))
    slots, n = {}, 0
    for e in seq:
        if e[0] in "MST":
            slots[e[:2]] = n % RING
            n += 1
    seq = [e for e in seq if e[0] not in "MT" or (next_max if e[2] == 1 else after_next)]
    return seq, slots


def last_unit(j):
    return max(n for n in range(NU) if UNITS[n][0] == j)


assert NU == 43
SEQ, SLOT = order(True, True)
BEFORE_LAST_SEQ, _ = order(True, False)
LAST_SEQ, _ = order(False, False)


def previous(seq, before, at):
    slot = SLOT[seq[at][:2]]
    for back, events in ((0, seq[:at]), (1, before)):
        for f in reversed(events):
            if f[0] in "MST" and SLOT[f[:2]] == slot:
                return f, back


NBLK = 39
SLOT_BLOCK = 2 * P
SLOTS = NBLK * SLOT_BLOCK
WCOLS = 3 * 1024
BOTH_AT = 12
EXP_AT = 14
ALL_SCALES = 9
ROUTED = 14 + 3 + 1 + 8 + 1 + 6 + 2 + 6


def attention(nc, psum, qT_d, kT_d, v_d, o_d, ident, ident_f, masks, pow2, w_all, xg_d, wts, escale, xhl, logits, rank_f, small, gates, slot_of, expert_of, xhl_id):
    with ExitStack() as ctx:
        def sb(name, shape, dt):
            return ctx.enter_context(nc.sbuf_tensor(name, shape, dt))

        def sem(name):
            return ctx.enter_context(nc.semaphore("at_" + name))

        kT = [sb(f"kT{n}", [P, 2, S], F16) for n in range(3)]
        qz = [sb(f"qz{n}", [P, GH, S], F16) for n in range(3)]
        vt = [sb(f"vt{n}", [P, NB, GH, 32], F32) for n in range(3)]
        probs = [sb(f"probs{n}", [P, GH, S - n * P], F32) for n in range(2)]
        row_max = sb("row_max", [P, 2, GH, NB], F32)
        neg_max = sb("neg_max", [P, P], F16)
        max_rows = sb("max_rows", [2 * GH * NB, P], F16)
        oT = sb("oT", [P, S], F32)
        den = sb("den", [P, NB, GH], F32)
        den2 = sb("den2", [P, NB, GH], F32)
        osb_all = sb("osb", [P, 3, NB, GH * HD], F32)
        osb = [osb_all[:, n] for n in range(3)]
        work = osb_all[:].rearrange("p n b d -> p (n b d)")
        sel = work[:, 0:4 * NT * E].rearrange("p (k t e) -> p k t e", k=4, t=NT)
        cnt = work[:, 4 * NT * E:5 * NT * E].rearrange("p (e t) -> p e t", e=E)

        load = [sem(f"load{n}") for n in range(3)]
        rows_in = [sem(f"rows_in{n}") for n in range(3)]
        o_out = [sem(f"o_out{n}") for n in range(3)]
        zeroed, m_ready, m_taken, s_ready, s_taken, v_done, neg1, neg2, turned, rows_copied, o_copied, o_turned, den_done, o_done, passed_, primed = (
            sem(n) for n in "zeroed m_ready m_taken s_ready s_taken v_done neg1 neg2 turned rows_copied o_copied o_turned den_done o_done passed primed".split())

        stage = sb("stage", [P, 3, 1024], F32)
        amax_w = sb("amax_w", [P, 3, E], F32)
        amax_k = sb("amax_k", [P, 2, 3], F32)
        pow2w = sb("pow2w", [P, 3], F32)
        rs = sb("rs", [P, 3], F32)
        rank_w = sb("rank_w", [P, 2, P], BF16)
        m = sb("m", [P, 8, NT], F32)
        both = sb("both", [P, NT, E], BF16)
        sones = sb("sones", [P, NBLK], F32)
        ex = sb("ex", [P, 4, E], F32)
        nbi = sb("nbi", [P, 2, E], I32)
        gef = sb("gef", [P, 2, NBLK], F32)
        gsc = sb("gsc", [P, 1], F32)
        stage_in = [sem(f"stage_in{n}") for n in range(3)]
        ids_moved, whole_max, ew_max, ew_all, ew_sum, ones_set, step_, ranked, exped, scattered, w_hi, w_lo, act_passed = (sem(n) for n in "ids_moved whole_max ew_max ew_all ew_sum ones_set route ranked exped scattered w_hi w_lo act_passed".split())

        bank = [psum[:, n, :] for n in range(8)]
        pv_view = psum[:, 6:8, :].rearrange("p b c -> p (b c)")
        ones = sb("ones", [P, 512], BF16)
        scales = sb("scales", [P, 3], F32)
        score_scale, value_scale = scales[:, 1:2], scales[:, 2:3]
        mask_l, mask_r = masks[:, 0], masks[:, 1:3]
        scaled = sem("scaled")

        def place(h):
            return h % 2 * 2 + h // 2

        pv = (bank[6], bank[7])

        def unit_view(slot, heads, w):
            return bank[slot][:, 0:len(heads) * w].rearrange("p (h w) -> p h w", w=w)

        block = ctx.enter_context(nc.Block())

        def walk(eng, step, between=lambda: None):
            with eng.Fori(0, 2) as i:
                for u in range(3):
                    step(Group(i, u), u, True, True, [Matrix(i, 12, 4 * u + n) for n in range(4)])
            between()
            with eng.Fori(0, 2) as i:
                for u in range(3):
                    step(Group(i, 6 + u), u, True, True, [Matrix(i, 6, 3 * E + 2 * u + n) for n in range(2)])
            for n in range(12, GROUPS):
                step(Group(None, n), n % 3, n + 1 < GROUPS, n + 2 < GROUPS, [Matrix(None, 0, 3 * E + 12 + 3 * (n - 12) + k) for k in range(3)])

        @block.sync
        def _(sp):
            def fetch(g, u):
                if g.loop is None:
                    b, pair = g.at // 4, g.at % 4 * 2
                else:
                    n = sp.snap(g.times(1))
                    b, pair = sp.snap(n // 4), sp.snap(n % 4 * 2)
                return b, pair

            def start(b, pair, u):
                cols = bass.ds(b * S, S)
                sp.dma_start(kT[u][:], kT_d[bass.ds(pair, 2), :, cols].rearrange("r p t -> p r t")).then_inc(load[u], 16)
                for k in range(2):
                    sp.dma_start(qz[u][64 * k:64 * k + 64, 2 * k:2 * k + 2, :],
                                 qT_d[bass.ds(pair, 2), 64 * k:64 * k + 64, cols].rearrange("r p t -> p r t")).then_inc(load[u], 16)
                sp.dma_start(vt[u][:], v_d[cols, bass.ds(pair * 64, GH * 32)].rearrange("(n p) d -> p n (d)", p=P)).then_inc(load[u], 16)

            def rows(g, u):
                for k in range(2):
                    for part in range(2):
                        r, n = 48 + 64 * k + part, (2 * k + part) * 2 * NB
                        sp.dma_start(qz[u][r:r + 1, 2 * k:2 * k + 2, :], max_rows[n:n + 2 * NB, :]).then_inc(rows_in[u], 16)

            def passed(g):
                if g.loop is not None:
                    sp.sem_inc(passed_, 1)
            for n in range(3):
                b, pair = fetch(Group(None, n), n)
                start(b, pair, n)
            for n in range(3):
                sp.sem_inc(o_out[n], 32 if n == 2 else 16)
            sp.wait_ge(rows_copied, 1)
            rows(Group(None, 0), 0)

            def step(g, u):
                ahead = live_fetch = None
                if g.loop is not None or g.at + 3 < GROUPS:
                    ahead = fetch(g + 3, u)
                if g.loop is not None or g.at >= 1:
                    prev = fetch(g + (-1), u)
                if g.loop is not None or g.at + 1 < GROUPS:
                    sp.wait_ge(rows_copied, g.times(1, 2))
                    passed(g)
                    rows(g + 1, (u + 1) % 3)
                if g.loop is not None or g.at >= 1:
                    sp.wait_ge(o_done, g.times(1, 1))
                    passed(g)
                    store(prev, (u - 1) % 3)
                if ahead is not None:
                    sp.wait_ge(v_done, g.times(NB, 2 * NB))
                    passed(g)
                    start(*ahead, u)

            def store(at, u):
                b, pair = at
                sp.dma_start(o_d[bass.ds(b * S, S), bass.ds(pair * 2 * HD, GH * HD)].rearrange("(n p) d -> p n d", p=P), osb[u]).then_inc(o_out[u], 16)
            step(Group(None, 0), 0)
            with sp.Fori(0, 4) as i:
                for u in (1, 2, 3):
                    step(Group(i, u), u % 3)
            for n in (13, 14, 15):
                step(Group(None, n), n % 3)
            sp.wait_ge(o_done, GROUPS + 1)
            store(fetch(Group(None, 15), 0), 0)
            sp.wait_ge(o_out[0], 16 * 7)
            sp.wait_ge(o_out[1], 16 * 6)
            sp.wait_ge(o_out[2], 16 * 7)

        @block.gpsimd
        def _(pool):
            pool.memset(ones[:], 1.0).then_inc(zeroed, 1)
            pool.memset(row_max[:, 1], -3e38).then_inc(ones_set, 1)
            pool.memset(sones[:], 1.0).then_inc(ones_set, 1)
            pool.tensor_copy(rank_w[:], rank_f[:]).then_inc(ones_set, 1)
            pool.memset(neg_max[:, P // 2:P], 0.0).then_inc(zeroed, 1)
            for n in range(3):
                for k in range(2):
                    pool.wait_ge(zeroed, 2 + 2 * n + k)
                    pool.memset(qz[n][64 - 64 * k:128 - 64 * k, 2 * k:2 * k + 2, :], 0.0).then_inc(zeroed, 1)
            pool.memset(probs[0][:, :, 0:2 * P], 0.0).then_inc(zeroed, 1)
            pool.memset(probs[1][:, :, 0:P], 0.0).then_inc(zeroed, 1)
            pool.wait_ge(step_, ROUTED)
            for k in range(2):
                if k == 1:
                    pool.wait_ge(scattered, 16 * NT)
                    pool.tensor_scalar(xhl_id, xhl_id, float(T), None, ALU.add).then_inc(ids_moved, 1)
                    pool.wait_ge(ids_moved, 1)
                for t in range(NT):
                    pool.indirect_dma_start(out=xg_d, out_offset=bass.IndirectOffsetOnAxis(ap=slot_of[:, k, t:t + 1], axis=0),
                                            in_=xhl[:, t, :], in_offset=None).then_inc(scattered, 16)
            pool.wait_ge(scattered, 16 * 2 * NT)
            pool.wait_ge(ew_all, 1)
            pool.partition_all_reduce(amax_k[:, 1], amax_k[:, 0], P, ABSMAX).then_inc(ew_sum, 1)

        @block.scalar
        def _(act):
            act.wait_ge(step_, EXP_AT)
            act.activation(m[:, 5], m[:, 4], ACT.Exp, scale=gsc[:]).then_inc(exped, 1)
            act.sem_inc(s_taken, NU)
            act.wait_ge(scaled, 3)

            def take_outputs(g, n):
                act.wait_ge(v_done, n)
                act.activation(oT[:], pv_view, ACT.Copy).then_inc(o_copied, 1)

            def load_stage(m):
                kind, c = m.kind, 4 if m.kind == 2 else 2
                if m.loop is not None:
                    act.sem_inc(act_passed, 1)
                act.dma_start(stage[:, kind].rearrange("p (c n) -> p c n", c=c),
                              wts[kind][bass.ds(m.expert(act), 1)].rearrange("e (c p) n -> p (e c) n", p=P)).then_inc(stage_in[kind], 16)

            def matrix(m):
                act.wait_ge(w_lo if m.splits else ew_max, m.times(1, 1 - (3 * E if m.splits else 0)))
                if m.loop is not None or m.at + 2 < 6 * E:
                    load_stage(m + 2)
                if m.splits:
                    act.wait_ge(stage_in[m.kind], m.turns(16, 16))
                    act.activation(w_all[:, m.expert(act), 0, m.kind * 1024:(m.kind + 1) * 1024], stage[:, m.kind], ACT.Copy,
                                   scale=rs[:, m.kind:m.kind + 1]).then_inc(w_hi, 1)

            def between():
                act.wait_ge(ew_all, ALL_SCALES)
                act.wait_ge(scattered, 16 * 2 * NT)
            act.sem_inc(ew_max, 1)
            act.sem_inc(w_lo, 1)
            for n in range(2):
                load_stage(Matrix(None, 0, n))

            def step(g, u, next_max, after_next, matrices):
                for k, (j, heads, q0, w) in enumerate(UNITS):
                    if k in SLOTS_OF[len(matrices)]:
                        matrix(matrices[SLOTS_OF[len(matrices)].index(k)])
                    if k == 6:
                        take_outputs(g, g.times(NB, NB))
                    if k == 0 or UNITS[k - 1][0] != j:
                        act.wait_ge(v_done, g.times(NB, NB + j - 1))
                    act.wait_ge(s_ready, g.times(NU, k + 1))
                    act.activation(probs[j % 2][:, heads[0]:heads[-1] + 1, q0:q0 + w], unit_view(SLOT["S", k], heads, w), ACT.Exp,
                                   scale=score_scale).then_inc(s_taken, 1)
            walk(act, step, between)
            take_outputs(None, NB * (GROUPS + 1))

        @block.vector
        def _(dve):
            def maxima(k, n):
                j, heads, k0, w = UNITS[k]
                i, half = NB - 1 - j, int(k0 > 0)
                dve.wait_ge(m_ready, n)
                view = unit_view(SLOT["M", k], heads, w)
                if len(heads) == GH:
                    into, view = row_max[:, 0, :, i].rearrange("p (k j) -> p j k", k=2), view.rearrange("p (j k) w -> p j k w", k=2)
                else:
                    into = row_max[:, half, place(heads[0]):place(heads[-1]) + 1:2, i]
                dve.tensor_reduce(into, view, AX, ALU.max).then_inc(m_taken, 1)

            def negate(n, last):
                dve.wait_ge(m_taken, last)
                dve.tensor_tensor(row_max[:, 0], row_max[:, 0], row_max[:, 1], ALU.max).then_inc(whole_max, 1)
                dve.wait_ge(whole_max, n)
                parts = neg_max[:, 0:P // 2].rearrange("p (k a m) -> p a k m", k=2, a=2)
                maxs = row_max[:, 0].rearrange("p (k j) n -> p k (j n)", k=2)
                dve.tensor_scalar(parts[:, 0], maxs, -2.0 ** -15, None, ALU.mult).then_inc(neg1, 1)
                dve.wait_ge(neg1, n)
                dve.scalar_tensor_tensor(out=parts[:, 1], in0=maxs, scalar=-2.0 ** -15, in1=parts[:, 0],
                                         op0=ALU.mult, op1=ALU.subtract).then_inc(neg2, 1)
                dve.wait_ge(neg2, n)

            def copy_rows(n):
                dve.wait_ge(turned, n)
                dve.tensor_copy(max_rows[:], bank[SLOT["T", 0]][0:64, 0:64].bitcast(F16)).then_inc(rows_copied, 1)

            def normalise(u, n, stored):
                dve.wait_ge(o_turned, n)
                both = pv_view.rearrange("p (n h d) -> p n h d", n=NB, h=GH)
                dve.reciprocal(den[:], both[:, :, :, HD]).then_inc(den_done, 1)
                dve.wait_ge(den_done, n * 2 - 1 if isinstance(n, int) else n * 2 - 1)
                dve.tensor_scalar(den2[:], den[:], value_scale, None, ALU.mult).then_inc(den_done, 1)
                dve.wait_ge(den_done, n * 2)
                dve.wait_ge(o_out[u], stored)
                dve.tensor_tensor(osb[u].rearrange("p n (h d) -> p n h d", h=GH), both[:, :, :, 0:HD],
                                  den2[:].rearrange("p n (h o) -> p n h o", o=1).broadcast_to([P, NB, GH, HD]), ALU.mult).then_inc(o_done, 1)

            def matrix(m):
                if m.splits:
                    e, at = m.expert(dve), slice(m.kind * 1024, (m.kind + 1) * 1024)
                    dve.wait_ge(w_hi, m.times(1, 1 - 3 * E))
                    dve.scalar_tensor_tensor(out=w_all[:, e, 1, at], in0=stage[:, m.kind], scalar=rs[:, m.kind:m.kind + 1],
                                             in1=w_all[:, e, 0, at], op0=ALU.mult, op1=ALU.subtract).then_inc(w_lo, 1)
                else:
                    dve.wait_ge(stage_in[m.kind], m.turns(16, 16))
                    dve.tensor_reduce(amax_w[:, m.kind, bass.ds(m.expert(dve), 1)], stage[:, m.kind], AX, ALU.max,
                                      apply_absolute_value=True).then_inc(ew_max, 1)

            def largest_of_all():
                dve.wait_ge(ew_max, 3 * E + 1)
                dve.tensor_reduce(amax_k[:, 0], amax_w[:], AX, ALU.max).then_inc(ew_all, 1)

            def scale_weights():
                dve.wait_ge(ew_sum, 1)
                dve.tensor_scalar(amax_k[:, 0], amax_k[:, 1], 2.0 ** -60, None, ALU.max).then_inc(ew_all, 1)
                dve.wait_ge(ew_all, 2)
                dve.tensor_scalar(pow2w[:].bitcast(U32), amax_k[:, 0].bitcast(U32), 0x7F800000, None, ALU.bitwise_and).then_inc(ew_all, 1)
                dve.wait_ge(ew_all, 3)
                dve.reciprocal(rs[:], pow2w[:]).then_inc(ew_all, 1)
                dve.tensor_scalar(escale[:, 0:1], pow2w[:, 0:1], 2.0 ** -25, None, ALU.mult).then_inc(ew_all, 1)
                dve.tensor_scalar(escale[:, 3:4], pow2w[:, 0:1], pow2w[:, 1:2], 2.0 ** -11, ALU.mult, ALU.mult).then_inc(ew_all, 1)
                dve.wait_ge(ew_all, 6)
                dve.tensor_scalar(escale[:, 1:2], rs[:, 0:1], 2.0 ** -28, None, ALU.mult).then_inc(ew_all, 1)
                dve.tensor_scalar(escale[:, 2:3], escale[:, 3:4], pow2w[:, 2:3], None, ALU.mult).then_inc(ew_all, 1)
                dve.wait_ge(ew_all, 8)
                dve.tensor_scalar(rs[:], rs[:], 2.0 ** 14, None, ALU.mult).then_inc(ew_all, 1)

            def route():
                dve.wait_ge(ones_set, 3)
                count = [0]
                incl = sel[:, 3].rearrange('p t e -> p (t e)').rearrange('p (e t) -> p e t', e=E)
                ge = sel[:, 0:2].rearrange('p k t e -> p (k t e)')[:, 0:NBLK * E].rearrange('p (b e) -> p b e', e=E)

                def link(ins):
                    count[0] += 1
                    ins.then_inc(step_, 1)
                    dve.wait_ge(step_, count[0])

                desc = small[:, 0:E].rearrange("p (o e) -> p o e", o=1).broadcast_to([P, NT, E])

                def wide(a):
                    return a.rearrange("p (t o) -> p t o", o=1).broadcast_to([P, NT, E])
                for k in range(2):
                    lg = logits[:] if k == 0 else sel[:, 2]
                    link(dve.tensor_reduce(m[:, k], lg, AX, ALU.max))
                    link(dve.tensor_tensor(sel[:, 3], lg, wide(m[:, k]), ALU.is_equal))
                    link(dve.tensor_tensor(sel[:, 3], sel[:, 3], desc, ALU.mult))
                    link(dve.tensor_reduce(m[:, 2 + k], sel[:, 3], AX, ALU.max))
                    link(dve.tensor_tensor(sel[:, k], desc, wide(m[:, 2 + k]), ALU.is_equal))
                    if k == 0:
                        link(dve.scalar_tensor_tensor(out=sel[:, 2], in0=sel[:, 0], scalar=-1e30, in1=logits[:], op0=ALU.mult, op1=ALU.add))
                link(dve.tensor_tensor(both[:], sel[:, 0], sel[:, 1], ALU.add))
                assert count[0] == BOTH_AT
                link(dve.tensor_scalar(gsc[:], pow2[:, 1:2], 2.0 ** -25, None, ALU.mult))
                link(dve.tensor_tensor(m[:, 4], m[:, 1], m[:, 0], ALU.subtract))
                assert count[0] == EXP_AT
                dve.wait_ge(exped, 1)
                link(dve.tensor_scalar(m[:, 6], m[:, 5], 1.0, None, ALU.add))
                link(dve.reciprocal(gates[:, 0], m[:, 6]))
                link(dve.tensor_tensor(gates[:, 1], gates[:, 0], m[:, 5], ALU.mult))
                dve.wait_ge(ranked, 1)
                link(dve.tensor_copy(cnt, bank[7][:, 0:NT * E].rearrange("p (t e) -> p e t", e=E)))
                for e in range(E):
                    link(dve.tensor_tensor_scan(incl[:, e, :], sones[:, 0:NT], cnt[:, e, :], 0.0, ALU.mult, ALU.add))
                link(dve.tensor_tensor(cnt, incl, cnt, ALU.subtract))
                link(dve.tensor_scalar(nbi[:, 0], incl[:, :, NT - 1], SLOT_BLOCK - 1.0, None, ALU.add))
                link(dve.tensor_scalar(nbi[:, 1], nbi[:, 0], SLOT_BLOCK.bit_length() - 1, None, ALU.arith_shift_right))
                link(dve.tensor_copy(ex[:, 0], nbi[:, 1]))
                link(dve.tensor_tensor_scan(ex[:, 1], sones[:, 0:E], ex[:, 0], 0.0, ALU.mult, ALU.add))
                link(dve.tensor_tensor(ex[:, 2], ex[:, 1], ex[:, 0], ALU.subtract))
                link(dve.tensor_scalar(ex[:, 3], ex[:, 2], float(SLOT_BLOCK), None, ALU.mult))
                link(dve.tensor_tensor(cnt, cnt, ex[:, 3].rearrange("p (e o) -> p e o", o=1).broadcast_to([P, E, NT]), ALU.add))
                link(dve.tensor_tensor(sel[:, 2], bank[6][:, 0:NT * E].rearrange("p (t e) -> p t e", e=E), cnt.rearrange("p e t -> p t e"), ALU.add))
                for k in range(2):
                    link(dve.tensor_tensor(sel[:, 3], sel[:, k], sel[:, 2], ALU.mult))
                    link(dve.tensor_reduce(m[:, 7], sel[:, 3], AX, ALU.add))
                    link(dve.tensor_copy(slot_of[:, k], m[:, 7]))
                assert count[0] == ROUTED, count
                link(dve.tensor_tensor(ge, small[:, E:E + NBLK].rearrange("p (b o) -> p b o", o=1).broadcast_to([P, NBLK, E]),
                                       ex[:, 1].rearrange("p (o e) -> p o e", o=1).broadcast_to([P, NBLK, E]), ALU.is_ge))
                link(dve.tensor_reduce(gef[:, 0], ge, AX, ALU.add))
                link(dve.tensor_scalar(gef[:, 1], gef[:, 0], E - 1.0, None, ALU.min))
                link(dve.tensor_copy(expert_of[:], gef[:, 1]))

            dve.tensor_scalar(scales[:, 0:1], pow2[:, 0:1], 2.0 ** -8, None, ALU.mult).then_inc(scaled, 1)
            dve.wait_ge(scaled, 1)
            dve.tensor_scalar(scales[:, 1:2], scales[:, 0:1], pow2[:, 0:1], None, ALU.mult).then_inc(scaled, 1)
            dve.tensor_scalar(scales[:, 2:3], pow2[:, 0:1], 2.0 ** -25, None, ALU.mult).then_inc(scaled, 1)
            route()
            for k in range(NU):
                maxima(k, k + 1)
            negate(1, NU)
            copy_rows(1)
            for k in range(LEAD):
                maxima(k, NU + k + 1)

            def between():
                largest_of_all()
                scale_weights()

            def step(g, u, next_max, after_next, matrices):
                for k in range(LEAD, NU):
                    if next_max:
                        maxima(k, g.times(NU, NU + k + 1))
                    for n, place_ in enumerate(SLOTS_OF[len(matrices)]):
                        if k == place_ + (10 if matrices[0].splits else 5):
                            matrix(matrices[n])
                    if k == LEAD + 9:
                        normalise((u - 1) % 3, g.times(1, 1), g.thirds(16, 16))
                if next_max:
                    negate(g.times(1, 2), g.times(NU, 2 * NU))
                for k in range(LEAD):
                    if after_next:
                        maxima(k, g.times(NU, 2 * NU + k + 1))
                    if k == 1 and next_max:
                        dve.wait_ge(rows_in[u], g.thirds(64, 64))
                        copy_rows(g.times(1, 2))
            walk(dve, step, between)
            normalise(0, GROUPS + 1, 16 * 6)

        @block.tensor
        def _(pe):
            def maxima(k, b):
                j, heads, k0, w = UNITS[k]
                i, ps = NB - 1 - j, bank[SLOT["M", k]]
                masked = k0 + w == S - P * j
                for n, h in enumerate(heads):
                    m = pe.matmul(ps[:, n * w:(n + 1) * w], qz[b][:, place(h), i * P:(i + 1) * P], kT[b][:, h // 2, k0:k0 + w], start=True, stop=not masked)
                    if masked:
                        m = pe.matmul(ps[:, (n + 1) * w - P:(n + 1) * w], mask_l, mask_r[:, 0, :], start=False, stop=True)
                m.then_inc(m_ready, 1)

            def scores(k, b):
                j, heads, q0, w = UNITS[k]
                ps = bank[SLOT["S", k]]
                for n, h in enumerate(heads):
                    m = pe.matmul(ps[:, n * w:(n + 1) * w], kT[b][:, h // 2, j * P:(j + 1) * P], qz[b][:, place(h), j * P + q0:j * P + q0 + w],
                                  start=True, stop=q0 > 0)
                    if q0 == 0:
                        m = pe.matmul(ps[:, n * w:n * w + P], mask_l, mask_r[:, 1, :], start=False, stop=True)
                m.then_inc(s_ready, 1)

            def values(j, piece, b):
                a, z = pieces(j)[piece]
                for lo in range(a - a % 512, z, 512):
                    c, q0, q1 = lo // 512, max(a, lo), min(z, lo + 512)
                    for h in range(GH):
                        m = pe.matmul(pv[c][32 * h:32 * h + 32, q0 - lo:q1 - lo], vt[b][:, j, h, :], probs[j % 2][:, h, q0 - P * j:q1 - P * j],
                                      start=(j == 0), stop=(j == 4 * c + 3))
                if z == S:
                    m.then_inc(v_done, 1)

            def turn_outputs(n):
                pe.wait_ge(o_copied, n)
                for i in range(NB):
                    m = pe.transpose(pv[i // 4][:, (i % 4) * P:(i % 4 + 1) * P], oT[:, i * P:(i + 1) * P], ident_f[:])
                m.then_inc(o_turned, 1)

            def turn_maxima(n):
                pe.wait_ge(neg2, n)
                pe.matmul(bank[SLOT["T", 0]][:, 0:64].bitcast(F16), neg_max[:], ident[:],
                          is_transpose=True, start=True, stop=True).then_inc(turned, 1)

            pe.wait_ge(ones_set, 3)
            pe.wait_ge(step_, BOTH_AT)
            pe.matmul(bank[6][:, 0:NT * E], rank_w[:, 0, :], both[:].rearrange("p t e -> p (t e)"), start=True, stop=True)
            pe.matmul(bank[7][:, 0:NT * E], rank_w[:, 1, :], both[:].rearrange("p t e -> p (t e)"), start=True, stop=True).then_inc(ranked, 1)
            pe.wait_ge(step_, ROUTED)
            pe.wait_ge(zeroed, 1)
            for c in range(2):
                m = pe.matmul(pv[c], ones[:, 0:P], ones[:], start=True, stop=c == 0)
            m.then_inc(v_done, NB - 2)
            pe.wait_ge(load[0], 64)
            pe.wait_ge(zeroed, 10)
            for k in range(NU):
                earlier = [n for n in range(k) if SLOT["M", n] == SLOT["M", k]]
                if earlier:
                    pe.wait_ge(m_taken, earlier[-1] + 1)
                maxima(k, 0)
            pe.wait_ge(m_taken, NU)
            turn_maxima(1)
            pe.wait_ge(rows_copied, 1)
            pe.wait_ge(load[1], 64)
            for k in range(LEAD):
                earlier = [n for n in range(k) if SLOT["M", n] == SLOT["M", k]]
                if earlier:
                    pe.wait_ge(m_taken, NU + earlier[-1] + 1)
                maxima(k, 1)
            pe.wait_ge(load[2], 64)

            def step(g, u, next_max, after_next, matrices):
                seq = SEQ if after_next else BEFORE_LAST_SEQ if next_max else LAST_SEQ
                before = SEQ if next_max else BEFORE_LAST_SEQ
                for at, (kind, k, x) in enumerate(seq):
                    if kind in "MST":
                        (pk, pn, px), back = previous(seq, before, at)
                        if pk == "M":
                            pe.wait_ge(m_taken, g.times(NU, NU * (px - back) + pn + 1))
                        elif pk == "S":
                            pe.wait_ge(s_taken, g.times(NU, NU * (1 - back) + pn + 1))
                        else:
                            pe.wait_ge(rows_copied, g.times(1, 2 - back))
                    if kind == "M":
                        if k == 0:
                            pe.wait_ge(load[(u + x) % 3], (g + x).thirds(64, 64))
                        maxima(k, (u + x) % 3)
                    elif kind == "T":
                        turn_maxima(g.times(1, 2))
                    elif kind == "S":
                        if k == 0:
                            pe.wait_ge(rows_in[u], g.thirds(64, 64))
                        scores(k, u)
                    elif kind == "O":
                        turn_outputs(g.times(1, 1))
                    elif k >= NB - 2:
                        pe.wait_ge(s_taken, g.times(NU, last_unit(k) + 1))
                        values(k, x, (u - 1) % 3)
                    else:
                        if k == 0 and x == 0:
                            pe.wait_ge(o_done, g.times(1, 1))
                        if x == 0:
                            pe.wait_ge(s_taken, g.times(NU, NU + last_unit(k) + 1))
                        values(k, x, u)
            walk(pe, step)
            for j in (NB - 2, NB - 1):
                pe.wait_ge(s_taken, NU * GROUPS + last_unit(j) + 1)
                values(j, 0, (GROUPS - 1) % 3)
            turn_outputs(GROUPS + 1)



class Half:

    def __init__(self, loop, at):
        self.loop, self.at = loop, at

    def __sub__(self, k):
        return Half(self.loop, self.at - k)

    def times(self, k, plus=0):
        return self.at * k + plus if self.loop is None else self.loop * (2 * k) + (self.at * k + plus)

    def halves(self, k, plus=0):
        n = self.at // 2 * k + plus
        return n if self.loop is None else self.loop * k + n


def experts(nc, psum, w_all, escale, expert_of, ident, xg_d, y_d, spare_rows, x, xs, late_in):
    with ExitStack() as ctx:
        def sb(name, shape, dt):
            return ctx.enter_context(nc.sbuf_tensor(name, shape, dt))

        def sem(name):
            return ctx.enter_context(nc.semaphore("ex_" + name))
        B2 = SLOT_BLOCK
        xg = sb("xg", [P, 2, 2, XCOLS], F16)
        row_of = sb("row_of", [P, 2, 2], I32)
        dump = sb("dump", [P, 2], F32)
        spare = sb("spare", [P, 2, 2], F32)
        xgT = sb("xgT", [P, 2, 4, B2], F16)
        sil = sb("sil", [P, 2, 2 * B2], F32)
        hf = sb("hf", [P, 2, 2 * B2], F32)
        hh = sb("hh", [P, 2, 4, B2], F16)
        hl = sb("hl", [P, 2, 4, B2], F16)
        ysb = sb("ysb", [P, 2, 2, D], F32)
        x_in = [sem(f"x_in{n}") for n in range(2)]
        y_out = [sem(f"y_out{n}") for n in range(2)]
        x_turned, xT_done, up_done, silu_done, h_done, hi_done, lo_done, down_done, y_done, spare_in, ids_seen, ids_taken, passed_, passed2 = (
            sem(n) for n in "x_turned xT_done up_done silu_done h_done hi_done lo_done down_done y_done spare_in ids_seen ids_taken passed passed2".split())
        ps_x = [psum[:, n, :].bitcast(F16).rearrange("p (c t) -> p c t", c=4) for n in (6, 7)]
        ps_1 = [psum[:, n, :] for n in (0, 1)]
        ps_3 = [psum[:, n, :] for n in (2, 3)]
        ps_y = [psum[:, n, :].rearrange("p (r d) -> p r d", r=2) for n in (4, 5)]
        block = ctx.enter_context(nc.Block())
        PEELED = 5
        assert (NBLK - PEELED) % 2 == 0

        def walk(eng, step):
            for n in range(PEELED):
                step(Half(None, n), n % 2)
            with eng.Fori(0, (NBLK - PEELED) // 2) as i:
                for u in range(2):
                    step(Half(i, PEELED + u), (PEELED + u) % 2)
            for n in range(NBLK, NBLK + 2):
                step(Half(None, n), n % 2)

        def live(n):
            return n.loop is not None or 0 <= n.at < NBLK

        def after(eng, signal, n):
            if not isinstance(n, int) or n > 0:
                eng.wait_ge(signal, n)

        @block.sync
        def _(sp):
            def passed(n):
                if n.loop is not None:
                    sp.sem_inc(passed_, 1)

            def step(n, u):
                if n.loop is None and n.at == 0:
                    sp.dma_start(spare[:], spare_rows).then_inc(spare_in, 16)
                ahead = n.times(B2) if n.loop is None else sp.snap(n.times(B2))
                if live(n):
                    after(sp, x_turned, n.times(1, -1))
                    after(sp, ids_taken, n.times(1, -1))
                    passed(n)
                    sp.dma_start(xg[:, u], xg_d[bass.ds(ahead, B2), :].rearrange("(r p) c -> p r c", p=P)).then_inc(x_in[u], 16)
                if n.loop is None and 1 <= n.at <= 4:
                    a, z = (n.at - 1) * NT // 4, n.at * NT // 4
                    sp.dma_start(xs[:, a:z], x[a * P:z * P, :].rearrange("(t p) d -> p t d", p=P)).then_inc(late_in, 16)
            walk(sp, step)
            sp.wait_ge(late_in, 64)

        @block.gpsimd
        def _(pool):
            def step(n, u):
                t = n - 2
                if live(t):
                    pool.wait_ge(ids_taken, t.times(1, 1))
                    pool.wait_ge(y_done, t.times(1, 1))
                    if t.loop is not None:
                        pool.sem_inc(passed2, 1)
                    for r in range(2):
                        pool.indirect_dma_start(out=y_d, out_offset=bass.IndirectOffsetOnAxis(ap=row_of[:, u, r:r + 1], axis=0),
                                                in_=ysb[:, u, r], in_offset=None).then_inc(y_out[u], 16)
            walk(pool, step)
            pool.wait_ge(y_out[0], 32 * ((NBLK + 1) // 2))
            pool.wait_ge(y_out[1], 32 * (NBLK // 2))

        @block.scalar
        def _(act):
            def step(n, u):
                t, b = n - 1, (u - 1) % 2

                def silu(half):
                    act.wait_ge(up_done, t.times(2, half + 1))
                    after(act, h_done, t.times(2, half - 1))
                    act.activation(sil[:, half], ps_1[half], ACT.Silu, scale=escale[:, 0:1]).then_inc(silu_done, 1)

                def hi(half):
                    act.wait_ge(h_done, t.times(2, half + 1))
                    after(act, down_done, t.times(1, -1))
                    act.activation(hh[:, b, 2 * half:2 * half + 2].rearrange("p c t -> p (c t)"), hf[:, half], ACT.Copy).then_inc(hi_done, 1)
                if live(t):
                    silu(0)
                    hi(0)
                    silu(1)
                if live(n):
                    act.wait_ge(x_turned, n.times(1, 1))
                    after(act, up_done, n.times(2, -2))
                    act.activation(xgT[:, u], ps_x[u], ACT.Copy).then_inc(xT_done, 1)
                if live(t):
                    hi(1)
                t = n - 2
                if live(t):
                    act.wait_ge(down_done, t.times(1, 1))
                    after(act, y_out[u], t.halves(32))
                    act.activation(ysb[:, u], ps_y[u], ACT.Copy, scale=escale[:, 2:3]).then_inc(y_done, 1)
            walk(act, step)

        @block.vector
        def _(dve):
            dve.wait_ge(spare_in, 16)

            def step(n, u):
                t, b = n - 1, (u - 1) % 2
                if live(t):
                    for half in range(2):
                        dve.wait_ge(silu_done, t.times(2, half + 1))
                        after(dve, lo_done, t.times(2, half - 1))
                        dve.scalar_tensor_tensor(out=hf[:, half], in0=ps_3[half], scalar=escale[:, 1:2], in1=sil[:, half], op0=ALU.mult, op1=ALU.mult).then_inc(h_done, 1)
                        dve.wait_ge(hi_done, t.times(2, half + 1))
                        dve.tensor_tensor(hl[:, b, 2 * half:2 * half + 2].rearrange("p c t -> p (c t)"), hf[:, half],
                                          hh[:, b, 2 * half:2 * half + 2].rearrange("p c t -> p (c t)"), ALU.subtract).then_inc(lo_done, 1)
                        if half == 0:
                            dve.wait_ge(x_in[b], t.halves(16, 16))
                            after(dve, y_out[b], t.halves(32))
                            rows = xg[:, b].bitcast(I32)[:, :, D]
                            dve.scalar_tensor_tensor(out=dump[:], in0=rows, scalar=0.0, in1=spare[:, b], op0=ALU.is_equal, op1=ALU.mult).then_inc(ids_seen, 1)
                            dve.wait_ge(ids_seen, t.times(1, 1))
                            dve.tensor_tensor(row_of[:, b], rows, dump[:], ALU.add).then_inc(ids_taken, 1)
            walk(dve, step)

        @block.tensor
        def _(pe):
            def step(n, u):
                t, b = n - 1, (u - 1) % 2
                if live(t):
                    e = pe.value_load(expert_of[0:1, bass.ds(t.times(1), 1)], min_val=0, max_val=E - 1)
                    pe.wait_ge(xT_done, t.times(1, 1))
                    for half in range(2):
                        after(pe, h_done, t.times(2, half - 1))
                        for w, ps in ((0, ps_1[half]), (1, ps_3[half])):
                            for c in range(2 * half, 2 * half + 2):
                                k_ = 0
                                for k in range(2):
                                    for (part, xo) in ((0, 0), (0, 2), (1, 0)):
                                        at = w * 1024 + k * 512 + c * P
                                        m = pe.matmul(ps[:, c % 2 * B2:(c % 2 + 1) * B2], w_all[:, e, part, at:at + P],
                                                      xgT[:, b, xo + k, :], start=k_ == 0, stop=k_ == 5)
                                        k_ += 1
                        m.then_inc(up_done, 1)
                if live(n):
                    pe.wait_ge(x_in[u], n.halves(16, 16))
                    after(pe, xT_done, n.times(1, -1))
                    for c in range(4):
                        for r in range(2):
                            m = pe.matmul(ps_x[u][:, c, r * P:(r + 1) * P], xg[:, u, r, c * P:(c + 1) * P], ident[:], is_transpose=True, start=True, stop=True)
                    m.then_inc(x_turned, 1)
                t = n - 2
                if live(t):
                    e = pe.value_load(expert_of[0:1, bass.ds(t.times(1), 1)], min_val=0, max_val=E - 1)
                    pe.wait_ge(lo_done, t.times(2, 2))
                    after(pe, y_done, t.times(1, -1))
                    for r in range(2):
                        k_ = 0
                        for c in range(4):
                            for (hx, part) in ((hh, 0), (hl, 0), (hh, 1)):
                                m = pe.matmul(ps_y[u][:, r], hx[:, u, c, r * P:(r + 1) * P], w_all[:, e, part, 2048 + c * D:2048 + (c + 1) * D], start=k_ == 0, stop=k_ == 11)
                                k_ += 1
                    m.then_inc(down_done, 1)
            walk(pe, step)


def ending(nc, psum, xs, o_d, y, y_d, woutt, out, ident_f, gates):
    with ExitStack() as ctx:
        def sb(name, shape, dt):
            return ctx.enter_context(nc.sbuf_tensor(name, shape, dt))

        def sem(name):
            return ctx.enter_context(nc.semaphore("en_" + name))
        wo = sb("wo", [P, 2, D], F32)
        os_ = sb("os", [P, 4, 2, D], F32)
        oT = sb("oTe", [P, 2, 2, 2, P], F32)
        f1 = sb("f1", [P, 2, 2, D], F32)
        f2 = sb("f2", [P, 2, 2, D], F32)
        sg = sb("sg", [P, 2, 2, D], F32)
        r1 = sb("r1", [P, 2, 2, D], F32)
        r2 = sb("r2", [P, 4, 2, D], F32)
        o_in = [sem(f"o_in{n}") for n in range(4)]
        y_in = [sem(f"y_in{n}") for n in range(4)]
        outs = [sem(f"out{n}") for n in range(4)]
        w_in, o_turned, oT_done, s_done, f1_done, f2_done, g_done, r1_done, r2_done, passed_ = (
            sem(n) for n in "w_in o_turned oT_done s_done f1_done f2_done g_done r1_done r2_done passed".split())
        ps_t = [psum[:, n, :] for n in (0, 1)]
        ps_s = [psum[:, n, :] for n in (2, 3)]
        block = ctx.enter_context(nc.Block())
        PAIRS = NT // 2
        PRODUCT, SILU, LAST, STORE = 1, 1, 2, 4

        def walk(eng, step):
            for n in range(4):
                step(Count(None, n), n)
            with eng.Fori(0, (PAIRS - 4) // 4) as i:
                for u in range(4):
                    step(Count(i, 4 + u), u)
            for n in range(PAIRS, PAIRS + STORE):
                step(Count(None, n), n % 4)

        def live(n):
            return n.loop is not None or 0 <= n.at < PAIRS

        def after(eng, signal, n):
            if not isinstance(n, int) or n > 0:
                eng.wait_ge(signal, n)

        @block.sync
        def _(sp):
            def passed(n):
                if n.loop is not None:
                    sp.sem_inc(passed_, 1)
            for n in range(4):
                sp.sem_inc(outs[n], 16)
            sp.dma_start(wo[:], woutt.rearrange("(c p) n -> p c n", p=P)).then_inc(w_in, 16)

            def step(n, u):
                t = n - STORE
                ahead, row = n.times(2 * P), t.times(2 * P)
                firsts, seconds = n.times(2 * P, 1), n.times(2 * P, 1 + T)
                if n.loop is not None:
                    ahead, row, firsts, seconds = sp.snap(ahead), sp.snap(row), sp.snap(firsts), sp.snap(seconds)

                def rows(of, at):
                    return of[bass.ds(at, 2 * P), :].rearrange("(j p) c -> p j c", p=P)
                if live(n):
                    after(sp, f2_done, n.times(2, -6))
                    passed(n)
                    after(sp, o_turned, n.times(1, -3))
                    passed(n)
                    sp.dma_start(os_[:, u], rows(o_d, ahead)).then_inc(o_in[u], 16)
                    sp.dma_start(y[:, u, 0], rows(y_d, firsts)).then_inc(y_in[u], 16)
                    sp.dma_start(y[:, u, 1], rows(y_d, seconds)).then_inc(y_in[u], 16)
                if live(t):
                    b = u
                    sp.wait_ge(r2_done, t.times(1, 1))
                    passed(t)
                    sp.dma_start(rows(out, row), r2[:, b]).then_inc(outs[b], 16)
            walk(sp, step)
            for n in range(4):
                sp.wait_ge(outs[n], 4 * PAIRS + 16)

        @block.scalar
        def _(act):
            def step(n, u):
                if live(n):
                    act.wait_ge(o_turned, n.times(1, 1))
                    after(act, s_done, n.times(1, -1))
                    act.activation(oT[:, u % 2].rearrange("p j c t -> p (j c t)"), ps_t[u % 2], ACT.Copy).then_inc(oT_done, 1)
                t, b = n - SILU, (u - SILU) % 2
                if live(t):
                    act.wait_ge(f2_done, t.times(2, 2))
                    after(act, r1_done, t.times(1, -1))
                    act.activation(sg[:, b], f2[:, b], ACT.Silu).then_inc(g_done, 1)
            walk(act, step)

        @block.vector
        def _(dve):
            def step(n, u):
                t, b = n - LAST, (u - LAST) % 4
                if live(n):
                    dve.wait_ge(y_in[u], n.quarters(32, 32))
                    for j in range(2):
                        dve.tensor_scalar(f1[:, u % 2, j], y[:, u, 0, j], gates[:, 0, bass.ds(n.times(2, j), 1)], None, ALU.mult).then_inc(f1_done, 1)
                if live(t):
                    dve.wait_ge(s_done, t.times(1, 1))
                    dve.wait_ge(g_done, t.times(1, 1))
                    dve.tensor_tensor(r1[:, b % 2].rearrange("p j d -> p (j d)"), ps_s[b % 2], sg[:, b % 2].rearrange("p j d -> p (j d)"), ALU.mult).then_inc(r1_done, 1)
                if live(n):
                    dve.wait_ge(f1_done, n.times(2, 2))
                    after(dve, g_done, n.times(1, -1))
                    for j in range(2):
                        dve.scalar_tensor_tensor(out=f2[:, u % 2, j], in0=y[:, u, 1, j], scalar=gates[:, 1, bass.ds(n.times(2, j), 1)], in1=f1[:, u % 2, j],
                                                 op0=ALU.mult, op1=ALU.add).then_inc(f2_done, 1)
                if live(t):
                    dve.wait_ge(r1_done, t.times(1, 1))
                    dve.wait_ge(outs[b], t.quarters(16, 16))
                    dve.tensor_tensor(r2[:, b], r1[:, b % 2], xs[:, bass.ds(t.times(2), 2)], ALU.add).then_inc(r2_done, 1)
            walk(dve, step)

        @block.tensor
        def _(pe):
            pe.wait_ge(w_in, 16)

            def step(n, u):
                if live(n):
                    pe.wait_ge(o_in[u], n.quarters(16, 16))
                    after(pe, oT_done, n.times(1, -1))
                    for j in range(2):
                        for c in range(2):
                            at = (2 * j + c) * P
                            m = pe.transpose(ps_t[u % 2][:, at:at + P], os_[:, u, j, c * P:(c + 1) * P], ident_f[:])
                    m.then_inc(o_turned, 1)
                t, b = n - PRODUCT, (u - PRODUCT) % 2
                if live(t):
                    pe.wait_ge(oT_done, t.times(1, 1))
                    after(pe, r1_done, t.times(1, -1))
                    for j in range(2):
                        for c in range(2):
                            m = pe.matmul(ps_s[b][:, j * D:(j + 1) * D], oT[:, b, j, c, :], wo[:, c, :], start=c == 0, stop=c == 1)
                    m.then_inc(s_done, 1)
            walk(pe, step)



def moe_attention_kernel(nc, x, wqkvg, w1t, w3t, w2t, woutt, rope_cos, rope_sin, ident16, ident32, mask_values, ranks_f, small, token_ids, spare_rows, out):
    def scratch(name, shape, dt):
        return nc.dram_tensor(name, shape, dt, kind="Internal").ap()
    qT_d, kT_d = scratch("qT_d", (H // 2, P, T), F16), scratch("kT_d", (H // 2, P, T), F16)
    v_d, o_d = scratch("v_d", (T, 32 * H), F32), scratch("o_d", (T, D), F32)
    xg_d, y_d = scratch("xg_d", (CLEARED * P * NT // 4, XCOLS), F16), scratch("y_d", (1 + 2 * T + 2 * SLOT_BLOCK, D), F32)
    assert SLOTS <= CLEARED * P * NT // 4
    with ExitStack() as ctx:
        def sb(name, shape, dt):
            return ctx.enter_context(nc.sbuf_tensor(name, shape, dt))
        psum = ctx.enter_context(nc.psum_tensor("psum", [P, 8, 512], F32))
        ident, ident_f, masks = sb("ident", [P, P], F16), sb("ident_f", [P, P], F32), sb("masks", [P, 3, P], BF16)
        logits, pow2 = sb("logits", [P, NT, E], F32), sb("pow2", [P, 2], F32)
        gates, slot_of = sb("gates", [P, 2, NT], F32), sb("slot_of", [P, 2, NT], I32)
        expert_of, escale = sb("expert_of", [P, NBLK], I32), sb("escale", [P, 4], F32)
        rank_f, small_sb = sb("rank_f", [P, 2, P], F32), sb("small_sb", [P, E + NBLK], F32)
        w_all = sb("w_all", [P, E, 2, WCOLS], F16)
        flat = w_all[:].rearrange("p e h w -> p (e h w)")
        xall = flat[:, 0:2 * NT * D].bitcast(F32).rearrange("p (t d) -> p t d", t=NT)
        xhl = flat[:, E * 2 * WCOLS - NT * XCOLS:].rearrange("p (t d) -> p t d", t=NT)
        xhl_id = flat.bitcast(I32)[:, (E * 2 * WCOLS - NT * XCOLS) // 2:].rearrange("p (t d) -> p t d", t=NT)[:, :, D]
        bank = [psum[:, n, :] for n in range(8)]
        experts_w = (w1t, w3t, w2t)
        project(nc, bank, x, wqkvg, rope_cos, rope_sin, ident16, ident32, mask_values, qT_d, kT_d, v_d, ident, ident_f, masks,
                xall, xhl, logits, pow2, xg_d, ranks_f, small, rank_f, small_sb, token_ids, xhl_id)
        attention(nc, psum, qT_d, kT_d, v_d, o_d, ident, ident_f, masks, pow2, w_all, xg_d, experts_w, escale, xhl, logits,
                  rank_f, small_sb, gates, slot_of, expert_of, xhl_id)
        xs, late_in = sb("xs", [P, NT, D], F32), ctx.enter_context(nc.semaphore("late_in"))
        experts(nc, psum, w_all, escale, expert_of, ident, xg_d, y_d, spare_rows, x, xs, late_in)
        y = flat[:, 0:4 * 2 * 2 * D * 2].bitcast(F32).rearrange("p (n k j d) -> p n k j d", n=4, k=2, j=2)
        ending(nc, psum, xs, o_d, y, y_d, woutt, out, ident_f, gates)


def constants():
    rate = 1.0 / 10000.0 ** (np.arange(0, HD, 2, dtype=np.float32) / HD)
    angle = np.outer(np.arange(S, dtype=np.float32), rate)
    angle = np.concatenate([angle, angle], axis=1)
    sign = np.tile([-1.0, 1.0], HD // 2)
    r = np.arange(P)
    masks = np.zeros((P, 3, P), np.float32)
    masks[:, 0] = np.eye(P) * 2.0 ** 60
    masks[:, 1] = np.where(r[None] > r[:, None], -2.0 ** 60, 0)
    masks[:, 2] = np.where(r[None] < r[:, None], -2.0 ** 60, 0)
    ranks = np.ones((P, 2, P), np.float32)
    ranks[:, 0] = r[:, None] < r[None]
    return {
        "rope_cos": np.tile((np.cos(angle) * 2.0 ** -22).astype(np.float32), (B, 1)),
        "rope_sin": np.tile((np.sin(angle) * sign * 2.0 ** -22).astype(np.float32), (B, 1)),
        "ident16": np.eye(P, dtype=np.float16), "ident32": np.eye(P, dtype=np.float32),
        "token_ids": (1 + np.arange(T).reshape(NT, P).T).astype(np.int32).copy(),
        "spare_rows": (1 + 2 * T + np.arange(4 * P).reshape(2, 2, P).transpose(2, 0, 1)).astype(np.float32).copy(),
        "mask_values": masks, "ranks_f": ranks,
        "small": np.tile(np.concatenate([E - np.arange(E), np.arange(NBLK)]).astype(np.float32), (P, 1)),
    }


def kernel(**inputs):
    import concourse.bacc as bacc
    from concourse.bass_utils import run_bass_kernel_spmd

    f = {k: np.asarray(v) for k, v in inputs.items()}
    arrays = {
        "x": np.ascontiguousarray(f["L0_attn_x"].reshape(T, D)),
        "wqkvg": np.ascontiguousarray(np.concatenate([f["L0_attn_Wqkv"].T, f["L0_ffn_gate_w"].T], axis=1)),
        "w1t": np.ascontiguousarray(f["L0_ffn_w1"].transpose(0, 2, 1)),
        "w3t": np.ascontiguousarray(f["L0_ffn_w3"].transpose(0, 2, 1)),
        "w2t": np.ascontiguousarray(f["L0_ffn_w2"].transpose(0, 2, 1)),
        "woutt": np.ascontiguousarray(f["L0_attn_Wout"].T),
        **constants(),
    }
    nc = bacc.Bacc("TRN2", target_bir_lowering=False, num_devices=1)
    args = {k: nc.dram_tensor("in_" + k, a.shape, mybir.dt.from_np(a.dtype), kind="ExternalInput").ap() for k, a in arrays.items()}
    out = nc.dram_tensor("out", (T, D), F32, kind="ExternalOutput").ap()
    moe_attention_kernel(nc, out=out, **args)
    r = run_bass_kernel_spmd(nc, [{"in_" + k: a for k, a in arrays.items()}], core_ids=[0])
    return r.results[0]["out"].reshape(B, S, D)
```
